# Optimizing a Trainium2 kernel written in Bass

```python
import numpy as np
import jax
import jax.numpy as jnp

def _softmax(x, axis=-1):
    return jax.nn.softmax(x, axis=axis)

def _gelu(x):
    return jax.nn.gelu(x, approximate=True)

def _silu(x):
    return jax.nn.silu(x)

def _sigmoid(x):
    return jax.nn.sigmoid(x)

def _layernorm(x, axis=-1, eps=1e-05):
    m = jnp.mean(x, axis=axis, keepdims=True)
    v = jnp.var(x, axis=axis, keepdims=True)
    return (x - m) / jnp.sqrt(v + eps)

def _scatter_add(tgt, idx, src, axis=0):
    return tgt.at[idx].add(src)

def _segment_sum(src, seg, n):
    return jax.ops.segment_sum(src, seg, n)
kernel_name = 'mk_dlrm_tower_d1_rec_r8_031a1e'

def setup_inputs(seed: int=0):
    np.random.seed(seed)
    _w = jnp.asarray

    def _rec_inputs():
        import jax
        import jax.numpy as jnp
        _tk = jax.random.key(seed)
        dense_ctx = jax.random.normal(jax.random.fold_in(_tk, 190), (1024, 16), jnp.float32)
        ids = jnp.stack([jax.random.randint(jax.random.fold_in(_tk, 200 + f), (1024,), 0, v, jnp.int32) for f, v in enumerate([1000, 1250, 1250, 1000, 1000, 1000, 1250, 12500, 1000, 1250, 12500, 1250, 12500, 12500, 12500, 12500])], axis=1)
        tbl_0 = 0.05 * jax.random.normal(jax.random.fold_in(_tk, 500 + 0), (1000, 256), jnp.float32)
        tbl_1 = 0.05 * jax.random.normal(jax.random.fold_in(_tk, 500 + 1), (1250, 256), jnp.float32)
        tbl_2 = 0.05 * jax.random.normal(jax.random.fold_in(_tk, 500 + 2), (1250, 256), jnp.float32)
        tbl_3 = 0.05 * jax.random.normal(jax.random.fold_in(_tk, 500 + 3), (1000, 256), jnp.float32)
        tbl_4 = 0.05 * jax.random.normal(jax.random.fold_in(_tk, 500 + 4), (1000, 256), jnp.float32)
        tbl_5 = 0.05 * jax.random.normal(jax.random.fold_in(_tk, 500 + 5), (1000, 256), jnp.float32)
        tbl_6 = 0.05 * jax.random.normal(jax.random.fold_in(_tk, 500 + 6), (1250, 256), jnp.float32)
        tbl_7 = 0.05 * jax.random.normal(jax.random.fold_in(_tk, 500 + 7), (12500, 256), jnp.float32)
        tbl_8 = 0.05 * jax.random.normal(jax.random.fold_in(_tk, 500 + 8), (1000, 256), jnp.float32)
        tbl_9 = 0.05 * jax.random.normal(jax.random.fold_in(_tk, 500 + 9), (1250, 256), jnp.float32)
        tbl_10 = 0.05 * jax.random.normal(jax.random.fold_in(_tk, 500 + 10), (12500, 256), jnp.float32)
        tbl_11 = 0.05 * jax.random.normal(jax.random.fold_in(_tk, 500 + 11), (1250, 256), jnp.float32)
        tbl_12 = 0.05 * jax.random.normal(jax.random.fold_in(_tk, 500 + 12), (12500, 256), jnp.float32)
        tbl_13 = 0.05 * jax.random.normal(jax.random.fold_in(_tk, 500 + 13), (12500, 256), jnp.float32)
        tbl_14 = 0.05 * jax.random.normal(jax.random.fold_in(_tk, 500 + 14), (12500, 256), jnp.float32)
        tbl_15 = 0.05 * jax.random.normal(jax.random.fold_in(_tk, 500 + 15), (12500, 256), jnp.float32)
        _rk = jax.random.fold_in(_tk, 7)
        W_top1 = 0.125 * jax.random.normal(jax.random.fold_in(_tk, 801), (64, 512), jnp.float32)
        W_top2 = 0.0441942 * jax.random.normal(jax.random.fold_in(_tk, 802), (512, 256), jnp.float32)
        W_top3 = 0.0625 * jax.random.normal(jax.random.fold_in(_tk, 803), (256, 1), jnp.float32)
        b_top1 = jnp.zeros((512,), jnp.float32)
        b_top2 = jnp.zeros((256,), jnp.float32)
        return (dense_ctx, ids, tbl_0, tbl_1, tbl_2, tbl_3, tbl_4, tbl_5, tbl_6, tbl_7, tbl_8, tbl_9, tbl_10, tbl_11, tbl_12, tbl_13, tbl_14, tbl_15, W_top1, b_top1, W_top2, b_top2, W_top3)
    dense_ctx, ids, tbl_0, tbl_1, tbl_2, tbl_3, tbl_4, tbl_5, tbl_6, tbl_7, tbl_8, tbl_9, tbl_10, tbl_11, tbl_12, tbl_13, tbl_14, tbl_15, W_top1, b_top1, W_top2, b_top2, W_top3 = _rec_inputs()

    def _L0_rec_setup():
        import jax, jax.numpy as jnp
        import numpy as np
        B, F, E = (512, 16, 256)
        N_LAYERS = 3
        key = jax.random.key(seed)
        k1, k2, k3 = jax.random.split(key, 3)
        x = jax.random.normal(k1, (B, F, E), dtype=jnp.float32)
        Ws = jax.random.normal(k2, (N_LAYERS, F, F * F), dtype=jnp.float32) * 0.05
        bs = jax.random.normal(k3, (N_LAYERS, F), dtype=jnp.float32) * 0.05
        return {'x': x, 'Ws': Ws, 'bs': bs}
    _L0_rec_all = _L0_rec_setup()
    _L0_rec_in = {k: v for k, v in _L0_rec_all.items() if k in ('Ws', 'bs')}
    del _L0_rec_all
    return {'dense_ctx': dense_ctx, 'ids': ids, 'tbl_0': tbl_0, 'tbl_1': tbl_1, 'tbl_2': tbl_2, 'tbl_3': tbl_3, 'tbl_4': tbl_4, 'tbl_5': tbl_5, 'tbl_6': tbl_6, 'tbl_7': tbl_7, 'tbl_8': tbl_8, 'tbl_9': tbl_9, 'tbl_10': tbl_10, 'tbl_11': tbl_11, 'tbl_12': tbl_12, 'tbl_13': tbl_13, 'tbl_14': tbl_14, 'tbl_15': tbl_15, 'W_top1': W_top1, 'b_top1': b_top1, 'W_top2': W_top2, 'b_top2': b_top2, 'W_top3': W_top3, 'L0_rec_Ws': _L0_rec_in['Ws'], 'L0_rec_bs': _L0_rec_in['bs']}

def reference(dense_ctx, ids, tbl_0, tbl_1, tbl_2, tbl_3, tbl_4, tbl_5, tbl_6, tbl_7, tbl_8, tbl_9, tbl_10, tbl_11, tbl_12, tbl_13, tbl_14, tbl_15, W_top1, b_top1, W_top2, b_top2, W_top3, L0_rec_Ws, L0_rec_bs):
    import jax
    import jax.numpy as jnp

    def _L0_rec_ref(x, Ws, bs):
        import jax, jax.numpy as jnp
        import numpy as np
        B, F, E = (512, 16, 256)
        N_LAYERS = 3
        B_, F_, E_ = x.shape
        n_layers = Ws.shape[0]
        xk = x
        outs = []
        for i in range(n_layers):
            z = jnp.einsum('bfe,bge->bfge', x, xk).reshape(B_, F_ * F_, E_)
            z = jnp.swapaxes(z, 1, 2)
            z = jnp.einsum('bcl,oc->bol', z, Ws[i]) + bs[i][None, :, None]
            z = jax.nn.relu(z)
            z = jnp.sum(z, axis=-1)
            outs.append(z)
            xk = jnp.broadcast_to(z[:, :, None], (B_, F_, E_))
        return jnp.concatenate(outs, axis=1)
    e = jnp.stack([tbl_0[ids[:, 0]], tbl_1[ids[:, 1]], tbl_2[ids[:, 2]], tbl_3[ids[:, 3]], tbl_4[ids[:, 4]], tbl_5[ids[:, 5]], tbl_6[ids[:, 6]], tbl_7[ids[:, 7]], tbl_8[ids[:, 8]], tbl_9[ids[:, 9]], tbl_10[ids[:, 10]], tbl_11[ids[:, 11]], tbl_12[ids[:, 12]], tbl_13[ids[:, 13]], tbl_14[ids[:, 14]], tbl_15[ids[:, 15]]], axis=1)
    z = _L0_rec_ref(e, L0_rec_Ws, L0_rec_bs)
    z = z.reshape(z.shape[0], -1)
    h = jnp.concatenate([z, dense_ctx], axis=1)
    h = jnp.maximum(h @ W_top1 + b_top1, 0.0)
    h = jnp.maximum(h @ W_top2 + b_top2, 0.0)
    y = h @ W_top3
    return y

_drawn_inputs = setup_inputs


def setup_inputs(seed=0):
    import zlib

    import numpy as np

    out = dict(_drawn_inputs(seed))
    spreads = {'b_top1': (0.0, 2.0), 'b_top2': (0.0, 2.0)}
    factors = {'dense_ctx': 8.0}
    for name, (base, spread) in spreads.items():
        noise = np.random.default_rng([zlib.crc32(name.encode()), seed]).standard_normal(out[name].shape)
        drawn = base * np.exp(spread * noise) if base else spread * noise
        out[name] = jnp.asarray(drawn.astype(out[name].dtype))
    for name, factor in factors.items():
        out[name] = (out[name] * factor).astype(out[name].dtype)
    return out
```

```python
from contextlib import ExitStack

import concourse.bass as bass
from concourse import mybir

ALU = mybir.AluOpType
ACT = mybir.ActivationFunctionType
F32 = mybir.dt.float32
BF16 = mybir.dt.bfloat16
I32 = mybir.dt.int32
AX_X = mybir.AxisListType.X

P = 128
B = 1024
F = 16
E = 256
HALVES = E // P
FE = HALVES * P
TILES = B // P
STEPS = F // 2
LAYERS = 3
CTX = 16
H_IN = LAYERS * F + CTX
H1 = 512
H2 = 256

MAIN = [4 * j for j in range(STEPS)]
FIRST_PAIR = [2 * j + sum(MAIN[:j]) for j in range(STEPS)]
ODD_PAIR = 2 * STEPS + sum(MAIN)
PAIRS = ODD_PAIR + STEPS
BANK = 32
BANKS = -(-PAIRS // BANK)
BANK_PAIRS = [min(BANK, PAIRS - BANK * k) for k in range(BANKS)]
RING = sum(MAIN[:6])
SLOT = [sum(MAIN[:j]) if j < 6 else sum(MAIN[6:j]) for j in range(STEPS)]
POOL_G = [0, 0, 1, 1, 2, 2, 3, 3]
N_DVE = STEPS - 1
N_POOL = sum(g > 0 for g in POOL_G) + 1
XBANKS = 4
SIGNAL_PAIRS = sorted({n - 1 for n in FIRST_PAIR[1:] + [ODD_PAIR, PAIRS] + [BANK * (k + 1) for k in range(BANKS - 1)]})
USED = [SIGNAL_PAIRS.index(n - 1) + 1 for n in FIRST_PAIR[1:] + [ODD_PAIR, PAIRS]]
FULL = [SIGNAL_PAIRS.index(min(BANK * (k + 1), PAIRS) - 1) + 1 for k in range(BANKS)]
N_USED = len(SIGNAL_PAIRS)


def pool_done(j):
    return sum(g > 0 for g in POOL_G[:j + 1])


def build(nc, dense_ctx, ids, tables, W_top1, b_top1, W_top2, b_top2, W_top3, Ws, bs, out):
    with ExitStack() as ctx:
        def sb(name, shape, dt=F32):
            return ctx.enter_context(nc.sbuf_tensor(name, shape, dt))

        def ps(name, shape, dt=F32):
            return ctx.enter_context(nc.psum_tensor(name, shape, dt))

        def sem(name):
            return ctx.enter_context(nc.semaphore(name))

        idx = sb("idx", [P, 2, F], I32)
        rows = sb("rows", [P, F, E])
        xt = sb("xt", [P, 2, F, FE])
        prod = sb("prod", [P, RING, FE])
        diag = sb("diag", [P, F, FE])
        odd = sb("odd", [P, STEPS, FE])
        relu0 = sb("relu0", [P, 2, BANK * F])
        part0 = sb("part0", [P, BANKS, F])
        y = sb("y", [P, 2, F // 2, F * F])
        h = sb("h", [P, 2, P])
        ident = sb("ident", [P, P])
        ones_bf = sb("ones_bf", [P, P], BF16)
        w_rows = sb("w_rows", [LAYERS * F, E])
        w0 = sb("w0", [P, HALVES, F])
        w0_half = sb("w0_half", [P, HALVES, F])
        w12 = sb("w12", [P, HALVES, 2 * F])
        bias_all = sb("bias_all", [P, LAYERS * F])
        bias_rest = sb("bias_rest", [P, 2, F])
        bias_part = sb("bias_part", [P, 3, F], BF16)
        bias_mat = sb("bias_mat", [P, PAIRS, F], BF16)
        vec_rows = sb("vec_rows", [8, P])
        vec = sb("vec", [P, 8])
        w1 = sb("w1", [H_IN, H1])
        w2 = sb("w2", [P, H1 // P, H2])
        h_t = sb("h_t", [H_IN, P])
        hid1 = sb("hid1", [P, H1 // P, P])
        hid2 = sb("hid2", [P, H2 // P, P])
        score = sb("score", [1, B])

        x_ps = [ps(f"x_ps{i}", [P, 2, FE]) for i in range(XBANKS)]
        acc = [ps(f"acc{i}", [P, BANK * F]) for i in range(2)]
        p_ps = ps("p_ps", [P, 2, F, F])
        mlp = ps("mlp", [P, H1])

        idx_loaded = [sem(f"idx_loaded{i}") for i in range(2)]
        ctx_loaded = [sem(f"ctx_loaded{i}") for i in range(2)]
        weights_loaded = sem("weights_loaded")
        rows_landed = [sem(f"rows_landed{j}") for j in range(STEPS)]
        zeroed = sem("zeroed")
        ident_ready = sem("ident_ready")
        ones_ready = sem("ones_ready")
        setup_turned = sem("setup_turned")
        setup_copied = sem("setup_copied")
        bias_step = sem("bias_step")
        turned = sem("turned")
        copied = sem("copied")
        squared = sem("squared")
        dve_mult = sem("dve_mult")
        pool_mult = sem("pool_mult")
        pairs_done = sem("pairs_done")
        acc_relued = sem("acc_relued")
        bank_summed = sem("bank_summed")
        z0_ready = sem("z0_ready")
        p_ready = sem("p_ready")
        y_ready = sem("y_ready")
        y_summed = sem("y_summed")
        h_turned = sem("h_turned")
        h_copied = sem("h_copied")
        hid1_ready = sem("hid1_ready")
        hid1_relued = sem("hid1_relued")
        hid2_ready = sem("hid2_ready")
        hid2_relued = sem("hid2_relued")
        score_ready = sem("score_ready")
        score_copied = sem("score_copied")
        out_written = sem("out_written")

        ids_t = ids.rearrange("(t p) f -> t p f", p=P)
        ctx_t = dense_ctx.rearrange("(t p) c -> t p c", p=P)

        def need(eng, semaphore, value):
            if not isinstance(value, int) or value > 0:
                eng.wait_ge(semaphore, value)

        def over_tiles(eng, tile):
            tile(0, 0)
            with eng.Fori(0, TILES // 2 - 1) as pair:
                tile(2 * pair + 1, 1)
                tile(2 * pair + 2, 0)
            tile(TILES - 1, 1)

        def loads(t, parity):
            return 8 * (t - parity) + 16

        def free_slots(eng, t, j):
            if j >= 6:
                eng.wait_ge(pairs_done, N_USED * t + (USED[3] if j == 6 else USED[5]))
            else:
                need(eng, pairs_done, N_USED * (t - 1) + (USED[6] if j < 4 else USED[7]))

        def is_first(t):
            return isinstance(t, int) and t == 0

        def is_last(t):
            return isinstance(t, int) and t == TILES - 1

        block = ctx.enter_context(nc.Block())

        @block.sync
        def _(sp):
            sp.dma_start(idx[:, 0, :], ids_t[0]).then_inc(idx_loaded[0], 16)
            sp.dma_start(idx[:, 1, :], ids_t[1]).then_inc(idx_loaded[1], 16)
            sp.dma_start(w_rows[:, :], Ws.rearrange("l o e -> (l o) e")).then_inc(weights_loaded, 16)
            sp.dma_start(vec_rows[0:4, :], b_top1.rearrange("(c p) -> c p", p=P)).then_inc(weights_loaded, 16)
            sp.dma_start(vec_rows[4:6, :], b_top2.rearrange("(c p) -> c p", p=P)).then_inc(weights_loaded, 16)
            sp.dma_start(vec_rows[6:8, :], W_top3.rearrange("(c p) o -> c (p o)", p=P)).then_inc(weights_loaded, 16)
            sp.dma_start(bias_all[:, :], bs.rearrange("l o -> (l o)").partition_broadcast(P)).then_inc(weights_loaded, 16)
            sp.dma_start(w1[:, :], W_top1).then_inc(weights_loaded, 16)
            sp.dma_start(w2[:, :, :], W_top2.rearrange("(c p) n -> p c n", p=P)).then_inc(weights_loaded, 16)
            sp.dma_start(h[:, 0, LAYERS * F:H_IN], ctx_t[0]).then_inc(ctx_loaded[0], 16)
            sp.dma_start(h[:, 1, LAYERS * F:H_IN], ctx_t[1]).then_inc(ctx_loaded[1], 16)

            def tile(t, parity):
                sp.wait_ge(turned, STEPS * t + STEPS)
                sp.dma_start(idx[:, parity, :], ids_t[t + 2]).then_inc(idx_loaded[parity], 16)
                sp.wait_ge(h_turned, t + 1)
                sp.dma_start(h[:, parity, LAYERS * F:H_IN], ctx_t[t + 2]).then_inc(ctx_loaded[parity], 16)

            with sp.Fori(0, TILES // 2 - 1) as pair:
                tile(2 * pair, 0)
                tile(2 * pair + 1, 1)
            sp.wait_ge(score_copied, TILES)
            sp.dma_start(out.rearrange("b o -> o b"), score[:, :]).then_inc(out_written, 16)
            sp.wait_ge(out_written, 16)

        @block.gpsimd
        def _(pool):
            pool.memset(ident[:, :], 0.0).then_inc(zeroed, 1)
            pool.wait_ge(zeroed, 1)
            pool.affine_select(out=ident[:, :], in_=ident[:, :], compare_op=ALU.not_equal, fill=1.0,
                               base=0, pattern=[[-1, P]], channel_multiplier=1).then_inc(ident_ready, 1)

            def gather(parity, j):
                for f in (2 * j, 2 * j + 1):
                    pool.indirect_dma_start(
                        out=rows[:, f, :], out_offset=None, in_=tables[f],
                        in_offset=bass.IndirectOffsetOnAxis(ap=idx[:, parity, f:f + 1], axis=0),
                    ).then_inc(rows_landed[j], 16)

            def multiply(t, parity, j):
                n = POOL_G[j]
                new_x = xt[:, parity, 2 * j:2 * j + 2, :]
                old_x = xt[:, parity, 0:n, :]
                out_ = prod[:, SLOT[j]:SLOT[j] + MAIN[j], :].rearrange("p (f g) e -> p f g e", f=2)[:, :, 0:n, :]
                if n == 1:
                    pool.tensor_tensor(out_[:, :, 0, :], old_x.to_broadcast([P, 2, FE]), new_x,
                                       ALU.mult).then_inc(pool_mult, 1)
                else:
                    pool.tensor_tensor(out_, old_x.unsqueeze(1).to_broadcast([P, 2, n, FE]),
                                       new_x.unsqueeze(2).to_broadcast([P, 2, n, FE]),
                                       ALU.mult).then_inc(pool_mult, 1)

            def tile(t, parity):
                gathered = 0
                for j in range(STEPS):
                    if POOL_G[j]:
                        if gathered == 0 and not is_last(t):
                            pool.wait_ge(idx_loaded[1 - parity], loads(t + 1, 1 - parity))
                        pool.wait_ge(copied, STEPS * t + j + 1)
                        free_slots(pool, t, j)
                        multiply(t, parity, j)
                        if not is_last(t):
                            for g in range(gathered, j + 1):
                                gather(1 - parity, g)
                            gathered = j + 1
                pool.wait_ge(copied, STEPS * t + STEPS)
                need(pool, pairs_done, N_USED * t)
                by_pair = xt[:, parity, :, :].rearrange("p (j two) e -> p j two e", two=2)
                pool.tensor_tensor(odd[:, :, :], by_pair[:, :, 0, :], by_pair[:, :, 1, :],
                                   ALU.mult).then_inc(pool_mult, 1)

            pool.wait_ge(idx_loaded[0], 16)
            for j in range(STEPS):
                gather(0, j)
            over_tiles(pool, tile)

        @block.scalar
        def _(act):
            act.wait_ge(setup_turned, 1)
            for half in range(HALVES):
                act.copy(w0[:, half, :], mlp[:, half * 64:half * 64 + F])
                act.mul(w0_half[:, half, :], mlp[:, half * 64:half * 64 + F], 0.5)
                act.copy(w12[:, half, :], mlp[:, half * 64 + F:half * 64 + 3 * F])
            act.copy(vec[:, :], mlp[:, P:P + 8]).then_inc(setup_copied, 1)

            def features(t, parity, j):
                act.wait_ge(turned, STEPS * t + j + 1)
                if j == 0 and not is_first(t) and not (isinstance(t, int) and t == 1):
                    act.wait_ge(p_ready, t - 1)
                act.copy(xt[:, parity, 2 * j:2 * j + 2, :], x_ps[j % XBANKS][:, :, :]).then_inc(copied, 1)
                if not is_first(t):
                    act.wait_ge(pairs_done, N_USED * (t - 1) + USED[j])
                act.activation(diag[:, 2 * j:2 * j + 2, :], x_ps[j % XBANKS][:, :, :], ACT.Square).then_inc(squared, 1)

            def relu_bank(t, parity, k):
                act.wait_ge(pairs_done, N_USED * t + FULL[k])
                need(act, bank_summed, BANKS * t + k - 1)
                n = BANK_PAIRS[k] * F
                act.activation(relu0[:, (BANKS * parity + k) % 2, 0:n], acc[(BANKS * parity + k) % 2][:, 0:n],
                               ACT.Relu, scale=2.0).then_inc(acc_relued, 1)

            def sum_layer(t, parity, layer, half):
                act.wait_ge(y_ready, 4 * t + 2 * (layer - 1) + half + 1)
                for i in range(F // 2):
                    o = layer * F + half * (F // 2) + i
                    last = act.activation(y[:, half, i, :], y[:, half, i, :], ACT.Relu,
                                          bias=bias_all[:, o:o + 1], accum_out=h[:, parity, o:o + 1])
                last.then_inc(y_summed, 1)

            def copy_h(t):
                act.wait_ge(h_turned, t + 1)
                need(act, hid1_ready, t)
                act.copy(h_t[:, :], mlp[0:H_IN, 0:P]).then_inc(h_copied, 1)

            def relu_hid1(t):
                act.wait_ge(hid1_ready, t + 1)
                need(act, hid2_ready, t)
                for c in range(H1 // P):
                    last = act.activation(hid1[:, c, :], mlp[:, c * P:(c + 1) * P], ACT.Relu, bias=vec[:, c:c + 1])
                last.then_inc(hid1_relued, 1)

            def relu_hid2(t):
                act.wait_ge(hid2_ready, t + 1)
                need(act, score_ready, t)
                for c in range(H2 // P):
                    last = act.activation(hid2[:, c, :], mlp[:, c * P:(c + 1) * P], ACT.Relu, bias=vec[:, 4 + c:5 + c])
                last.then_inc(hid2_relued, 1)

            def copy_score(t):
                act.wait_ge(score_ready, t + 1)
                act.copy(score[:, bass.ts(t, P)], mlp[0:1, 0:P]).then_inc(score_copied, 1)

            def tile(t, parity):
                first = is_first(t)
                second = isinstance(t, int) and t == 1
                for j in range(STEPS):
                    if j + 3 < STEPS:
                        features(t, parity, j + 3)
                    elif not is_last(t):
                        features(t + 1, 1 - parity, j + 3 - STEPS)
                    if not first:
                        if j == 0:
                            relu_bank(t - 1, 1 - parity, 3)
                            relu_bank(t - 1, 1 - parity, 4)
                        if j == 3:
                            sum_layer(t - 1, 1 - parity, 1, 0)
                        if j == 4:
                            sum_layer(t - 1, 1 - parity, 1, 1)
                    if j == 5:
                        relu_bank(t, parity, 0)
                    if j == 6:
                        relu_bank(t, parity, 1)
                    if j == 7:
                        relu_bank(t, parity, 2)
                        if not first:
                            sum_layer(t - 1, 1 - parity, 2, 0)
                            sum_layer(t - 1, 1 - parity, 2, 1)
                if not first:
                    copy_h(t - 1)
                    relu_hid1(t - 1)
                    relu_hid2(t - 1)
                    copy_score(t - 1)

            for j in range(3):
                features(0, 0, j)
            over_tiles(act, tile)
            t = TILES - 1
            relu_bank(t, 1, 3)
            relu_bank(t, 1, 4)
            for layer in (1, 2):
                for half in range(2):
                    sum_layer(t, 1, layer, half)
            copy_h(t)
            relu_hid1(t)
            relu_hid2(t)
            copy_score(t)

        @block.vector
        def _(dve):
            dve.memset(h[:, :, H_IN:P], 0.0)
            dve.memset(ones_bf[:, :], 1.0).then_inc(ones_ready, 1)
            dve.memset(bias_mat[:, :, :], 0.0).then_inc(bias_step, 1)
            dve.wait_ge(weights_loaded, 16 * 7)
            steps = [1]

            def link(instruction):
                instruction.then_inc(bias_step, 1)
                steps[0] += 1
                dve.wait_ge(bias_step, steps[0])

            link(dve.tensor_copy(bias_part[:, 0, :], bias_all[:, 0:F]))
            link(dve.tensor_tensor(bias_rest[:, 0, :], bias_all[:, 0:F], bias_part[:, 0, :], ALU.subtract))
            link(dve.tensor_copy(bias_part[:, 1, :], bias_rest[:, 0, :]))
            link(dve.tensor_tensor(bias_rest[:, 1, :], bias_rest[:, 0, :], bias_part[:, 1, :], ALU.subtract))
            link(dve.tensor_copy(bias_part[:, 2, :], bias_rest[:, 1, :]))
            for i in range(3):
                row = slice(32 * i, 32 * i + 1)
                part = bias_part[row, i:i + 1, :]
                link(dve.tensor_copy(bias_mat[row, :, :], part.to_broadcast([1, PAIRS, F])))
                for j in range(STEPS):
                    last = dve.tensor_scalar(bias_mat[row, FIRST_PAIR[j]:FIRST_PAIR[j] + 2, :],
                                             part.to_broadcast([1, 2, F]), 0.5, None, ALU.mult)
                link(last)

            def multiply(t, parity, j):
                dve.wait_ge(copied, STEPS * t + j + 1)
                dve.wait_ge(squared, STEPS * t + j + 1)
                free_slots(dve, t, j)
                g0, g1 = POOL_G[j], 2 * j
                n = g1 - g0
                out_ = prod[:, SLOT[j]:SLOT[j] + MAIN[j], :].rearrange("p (f g) e -> p f g e", f=2)[:, :, g0:g1, :]
                a = xt[:, parity, g0:g1, :].unsqueeze(1).to_broadcast([P, 2, n, FE])
                b = x_ps[j % XBANKS][:, :, :].unsqueeze(2).to_broadcast([P, 2, n, FE])
                dve.tensor_tensor(out_, a, b, ALU.mult).then_inc(dve_mult, 1)

            def sum_bank(t, parity, k):
                dve.wait_ge(acc_relued, BANKS * t + k + 1)
                n = BANK_PAIRS[k]
                dve.tensor_reduce(part0[:, k, :],
                                  relu0[:, (BANKS * parity + k) % 2, 0:n * F].rearrange("p (n o) -> p o n", o=F),
                                  AX_X, ALU.add).then_inc(bank_summed, 1)

            def sum_layer0(t, parity):
                dve.wait_ge(bank_summed, BANKS * (t + 1))
                dve.wait_ge(ctx_loaded[parity], loads(t, parity))
                dve.tensor_reduce(h[:, parity, 0:F], part0[:, :, :].rearrange("p k o -> p o k"),
                                  AX_X, ALU.add).then_inc(z0_ready, 1)

            def scale_layer(t, parity, layer, half):
                if half == 0:
                    if layer == 1:
                        dve.wait_ge(z0_ready, t + 1)
                        dve.wait_ge(p_ready, t + 1)
                    else:
                        dve.wait_ge(y_summed, 4 * t + 2)
                if layer == 1:
                    need(dve, y_summed, 4 * t)
                ho = F // 2
                a = p_ps[:, layer - 1, half * ho:(half + 1) * ho, :].rearrange("p o f -> p (o f)")
                b = h[:, parity, (layer - 1) * F:layer * F]
                dve.tensor_tensor(y[:, half, :, :].rearrange("p o (f g) -> p (o f) g", g=F),
                                  a.unsqueeze(2).to_broadcast([P, ho * F, F]),
                                  b.unsqueeze(1).to_broadcast([P, ho * F, F]), ALU.mult).then_inc(y_ready, 1)

            def tile(t, parity):
                first = is_first(t)
                for j in range(STEPS):
                    if j > 0:
                        multiply(t, parity, j)
                    if not first:
                        if j == 1:
                            sum_bank(t - 1, 1 - parity, 2)
                        if j == 2:
                            sum_bank(t - 1, 1 - parity, 3)
                            sum_bank(t - 1, 1 - parity, 4)
                            sum_layer0(t - 1, 1 - parity)
                            scale_layer(t - 1, 1 - parity, 1, 0)
                        if j == 3:
                            scale_layer(t - 1, 1 - parity, 1, 1)
                        if j == 6:
                            scale_layer(t - 1, 1 - parity, 2, 0)
                            scale_layer(t - 1, 1 - parity, 2, 1)
                    if j == 6:
                        sum_bank(t, parity, 0)
                    if j == 7:
                        sum_bank(t, parity, 1)

            over_tiles(dve, tile)
            t = TILES - 1
            for k in (2, 3, 4):
                sum_bank(t, 1, k)
            sum_layer0(t, 1)
            for layer in (1, 2):
                for half in range(2):
                    scale_layer(t, 1, layer, half)

        @block.tensor
        def _(pe):
            pe.wait_ge(weights_loaded, 16 * 7)
            pe.wait_ge(ident_ready, 1)
            for half in range(HALVES):
                pe.transpose(mlp[:, half * 64:half * 64 + LAYERS * F], w_rows[:, half * P:(half + 1) * P],
                             ident[0:LAYERS * F, 0:LAYERS * F])
            pe.transpose(mlp[:, P:P + 8], vec_rows[:, :], ident[0:8, 0:8]).then_inc(setup_turned, 1)

            def turn(t, j):
                pe.wait_ge(rows_landed[j], 32 * t + 32)
                q = STEPS * t + j - XBANKS
                if not (isinstance(t, int) and q < 0):
                    before = t if j >= XBANKS else t - 1
                    jb = (j - XBANKS) % STEPS
                    if jb > 0:
                        pe.wait_ge(dve_mult, N_DVE * before + jb)
                    pe.wait_ge(squared, STEPS * before + jb + 1)
                for f in range(2):
                    for half in range(HALVES):
                        last = pe.transpose(x_ps[j % XBANKS][:, f, half * P:(half + 1) * P],
                                            rows[:, 2 * j + f, half * P:(half + 1) * P], ident[:, :])
                last.then_inc(turned, 1)

            def contract(t, parity, n, lhs, weights):
                k, c = divmod(n, BANK)
                bank = acc[(BANKS * parity + k) % 2]
                if c == 0:
                    need(pe, acc_relued, BANKS * t + k - 1)
                    pe.matmul(bank[:, 0:BANK_PAIRS[k] * F], ones_bf[:, :],
                              bias_mat[:, n:n + BANK_PAIRS[k], :].rearrange("p n o -> p (n o)"),
                              start=True, stop=False)
                for half in range(HALVES):
                    last = pe.matmul(bank[:, c * F:(c + 1) * F], lhs[:, half * P:(half + 1) * P],
                                     weights[:, half, :], start=False,
                                     stop=(c == BANK_PAIRS[k] - 1 and half == HALVES - 1))
                if n in SIGNAL_PAIRS:
                    last.then_inc(pairs_done, 1)

            def step_pairs(t, parity, j):
                pe.wait_ge(squared, STEPS * t + j + 1)
                for f in range(2):
                    contract(t, parity, FIRST_PAIR[j] + f, diag[:, 2 * j + f, :], w0_half)
                if j > 0:
                    pe.wait_ge(dve_mult, N_DVE * t + j)
                if POOL_G[j]:
                    pe.wait_ge(pool_mult, N_POOL * t + pool_done(j))
                for i in range(MAIN[j]):
                    contract(t, parity, FIRST_PAIR[j] + 2 + i, prod[:, SLOT[j] + i, :], w0)

            def odd_pairs(t, parity):
                pe.wait_ge(pool_mult, N_POOL * t + N_POOL)
                for i in range(STEPS):
                    contract(t, parity, ODD_PAIR + i, odd[:, i, :], w0)

            def project(t, parity):
                pe.wait_ge(copied, STEPS * t + STEPS)
                need(pe, y_ready, 4 * t)
                for f in range(F):
                    for half in range(HALVES):
                        last = pe.matmul(p_ps[:, :, :, f].rearrange("p l o -> p (l o)"),
                                         xt[:, parity, f, half * P:(half + 1) * P], w12[:, half, :],
                                         start=(f == 0 and half == 0), stop=(f == F - 1 and half == HALVES - 1))
                last.then_inc(p_ready, 1)

            def turn_h(t, parity):
                pe.wait_ge(z0_ready, t + 1)
                pe.wait_ge(y_summed, 4 * t + 4)
                pe.wait_ge(ctx_loaded[parity], loads(t, parity))
                need(pe, score_copied, t)
                pe.transpose(mlp[:, 0:P], h[:, parity, :], ident[:, :]).then_inc(h_turned, 1)

            def top1(t):
                pe.wait_ge(h_copied, t + 1)
                for c in range(H1 // P):
                    last = pe.matmul(mlp[:, c * P:(c + 1) * P], w1[:, c * P:(c + 1) * P], h_t[:, :],
                                     start=True, stop=True)
                last.then_inc(hid1_ready, 1)

            def top2(t):
                pe.wait_ge(hid1_relued, t + 1)
                for m in range(H2 // P):
                    for c in range(H1 // P):
                        last = pe.matmul(mlp[:, m * P:(m + 1) * P], w2[:, c, m * P:(m + 1) * P], hid1[:, c, :],
                                         start=(c == 0), stop=(c == H1 // P - 1))
                last.then_inc(hid2_ready, 1)

            def top3(t):
                pe.wait_ge(hid2_relued, t + 1)
                for c in range(H2 // P):
                    last = pe.matmul(mlp[0:1, 0:P], vec[:, 6 + c:7 + c], hid2[:, c, :],
                                     start=(c == 0), stop=(c == H2 // P - 1))
                last.then_inc(score_ready, 1)

            def tile(t, parity):
                first = is_first(t)
                second = isinstance(t, int) and t == 1
                for j in range(STEPS):
                    if j + 3 < STEPS:
                        turn(t, j + 3)
                    elif not is_last(t):
                        turn(t + 1, j + 3 - STEPS)
                    step_pairs(t, parity, j)
                odd_pairs(t, parity)
                project(t, parity)
                if not first:
                    turn_h(t - 1, 1 - parity)
                    top1(t - 1)
                    top2(t - 1)
                    top3(t - 1)

            for j in range(3):
                turn(0, j)
            pe.wait_ge(setup_copied, 1)
            pe.wait_ge(ones_ready, 1)
            pe.wait_ge(bias_step, 1 + 5 + 6)
            over_tiles(pe, tile)
            t = TILES - 1
            turn_h(t, 1)
            top1(t)
            top2(t)
            top3(t)


_TABLES = [f"tbl_{f}" for f in range(F)]
_INS = ["dense_ctx", "ids", *_TABLES, "W_top1", "b_top1", "W_top2", "b_top2", "W_top3", "L0_rec_Ws", "L0_rec_bs"]


def kernel(**inputs):
    import numpy as np
    import concourse.bacc as bacc
    from concourse.bass_utils import run_bass_kernel_spmd

    nc = bacc.Bacc("TRN2", target_bir_lowering=False, num_devices=1)
    arrays, args = {}, {}
    for name in _INS:
        a = np.ascontiguousarray(inputs[name])
        arrays[f"in_{name}"] = a
        args[name] = nc.dram_tensor(f"in_{name}", a.shape, mybir.dt.from_np(a.dtype), kind="ExternalInput").ap()
    out = nc.dram_tensor("out", (B, 1), F32, kind="ExternalOutput").ap()
    build(nc, args["dense_ctx"], args["ids"], [args[n] for n in _TABLES], args["W_top1"], args["b_top1"],
          args["W_top2"], args["b_top2"], args["W_top3"], args["L0_rec_Ws"], args["L0_rec_bs"], out)
    r = run_bass_kernel_spmd(nc, [arrays], core_ids=[0])
    return r.results[0]["out"]
```

```python
from contextlib import ExitStack

import concourse.bass as bass
from concourse import mybir

ALU = mybir.AluOpType
ACT = mybir.ActivationFunctionType
F32 = mybir.dt.float32
I32 = mybir.dt.int32
AX_X = mybir.AxisListType.X

P = 128
B = 1024
F = 16
E = 256
HALVES = E // P
FE = HALVES * P
TILES = B // P
STEPS = F // 2
LAYERS = 3
CTX = 16
H_IN = LAYERS * F + CTX
H1 = 512
H2 = 256

MAIN = [4 * j for j in range(STEPS)]
RING = sum(MAIN[:STEPS - 1])
SLOT = [sum(MAIN[:j]) if j < STEPS - 1 else 0 for j in range(STEPS)]
GROUP = 4
GROUP_SLOT = [SLOT[j] + GROUP * i for j in range(STEPS) for i in range(MAIN[j] // GROUP)]
ROUNDS = len(GROUP_SLOT) // 4
ROUND_STEP = [min(j for j in range(STEPS) if sum(MAIN[:j + 1]) >= 4 * GROUP * (r + 1)) for r in range(ROUNDS)]
DIAG_ROUND = ROUNDS
ODD_ROUND = ROUNDS + 1
N_ROUND = ROUNDS + 2
BANKS = 5
BANK_ROUND = [1, 3, 5, DIAG_ROUND, ODD_ROUND]
BANK_COLS = [GROUP * P] * 4 + [2 * P]
SUM_SLOTS = sum(BANK_COLS) // P
POOL_G = [0, 0, 1, 1, 2, 2, 3, 3]
N_DVE = STEPS - 1
N_POOL = sum(g > 0 for g in POOL_G) + 1
XBANKS = 4
ACC_OF_BANK = [0, 1, 1, 0, 1]
ACC_OF_PT = 0
SETUP_STEPS = 10


def pool_done(j):
    return sum(g > 0 for g in POOL_G[:j + 1])


def last_round(slots):
    groups = [i for i, s in enumerate(GROUP_SLOT) if s in slots]
    return max(i for i in groups if i < (sum(MAIN[:STEPS - 1]) // GROUP)) // 4


def last_round_any(slots):
    return max(i for i, s in enumerate(GROUP_SLOT) if s in slots) // 4


def build(nc, dense_ctx, ids, tables, W_top1, b_top1, W_top2, b_top2, W_top3, Ws, bs, out):
    with ExitStack() as ctx:
        def sb(name, shape, dt=F32):
            return ctx.enter_context(nc.sbuf_tensor(name, shape, dt))

        def ps(name, shape, dt=F32):
            return ctx.enter_context(nc.psum_tensor(name, shape, dt))

        def sem(name):
            return ctx.enter_context(nc.semaphore(name))

        idx = sb("idx", [P, 2, F], I32)
        rows = sb("rows", [P, F, E])
        xt = sb("xt", [P, 2, F, FE])
        prod = sb("prod", [P, RING, FE])
        diag = sb("diag", [P, F, FE])
        odd = sb("odd", [P, STEPS, FE])
        relu0 = sb("relu0", [P, SUM_SLOTS, P])
        pt = sb("pt", [P, GROUP * P])
        y = sb("y", [P, 2, F // 4, F // 2, 4 * F])
        h = sb("h", [P, 2, P])
        ident = sb("ident", [P, P])
        fold = sb("fold", [P, F])
        second = sb("second", [P, 1])
        w_rows = sb("w_rows", [LAYERS * F, E])
        w0 = sb("w0", [P, HALVES, 2, 2 * F])
        w0_half = sb("w0_half", [P, HALVES, 2 * F])
        w12 = sb("w12", [P, HALVES, 2 * F])
        bias_all = sb("bias_all", [P, LAYERS * F])
        bias_masked = sb("bias_masked", [P, F])
        bias0 = sb("bias0", [P, 1])
        bias0_2nd = sb("bias0_2nd", [P, 1])
        bias_bank = sb("bias_bank", [P, 3])
        vec_rows = sb("vec_rows", [8, P])
        vec = sb("vec", [P, 8])
        w1 = sb("w1", [H_IN, H1])
        w2 = sb("w2", [P, H1 // P, H2])
        h_t = sb("h_t", [H_IN, P])
        hid1 = sb("hid1", [P, H1 // P, P])
        hid2 = sb("hid2", [P, H2 // P, P])
        score = sb("score", [1, B])

        x_ps = [ps(f"x_ps{i}", [P, 2, FE]) for i in range(XBANKS)]
        acc = [ps(f"acc{i}", [P, GROUP * P]) for i in range(2)]
        p_ps = ps("p_ps", [P, F // 4, 2, F, 4])
        mlp = ps("mlp", [P, H1])

        idx_loaded = [sem(f"idx_loaded{i}") for i in range(2)]
        ctx_loaded = [sem(f"ctx_loaded{i}") for i in range(2)]
        weights_loaded = sem("weights_loaded")
        rows_landed = [sem(f"rows_landed{j}") for j in range(STEPS)]
        zeroed = sem("zeroed")
        ident_ready = sem("ident_ready")
        setup_turned = sem("setup_turned")
        setup_copied = sem("setup_copied")
        setup_step = sem("setup_step")
        turned = sem("turned")
        copied = sem("copied")
        squared = sem("squared")
        dve_mult = sem("dve_mult")
        pool_mult = sem("pool_mult")
        rounds_done = sem("rounds_done")
        projected = sem("projected")
        relued = sem("relued")
        pt_copied = sem("pt_copied")
        z0_summed = sem("z0_summed")
        z0_ready = sem("z0_ready")
        p_ready = sem("p_ready")
        y_ready = sem("y_ready")
        y_summed = sem("y_summed")
        h_turned = sem("h_turned")
        h_copied = sem("h_copied")
        hid1_ready = sem("hid1_ready")
        hid1_relued = sem("hid1_relued")
        hid2_ready = sem("hid2_ready")
        hid2_relued = sem("hid2_relued")
        score_ready = sem("score_ready")
        score_copied = sem("score_copied")
        out_written = sem("out_written")

        ids_t = ids.rearrange("(t p) f -> t p f", p=P)
        ctx_t = dense_ctx.rearrange("(t p) c -> t p c", p=P)

        def need(eng, semaphore, value):
            if not isinstance(value, int) or value > 0:
                eng.wait_ge(semaphore, value)

        def over_tiles(eng, tile):
            tile(0, 0)
            tile(1, 1)
            with eng.Fori(0, TILES // 2 - 2) as pair:
                tile(2 * pair + 2, 0)
                tile(2 * pair + 3, 1)
            tile(TILES - 2, 0)
            tile(TILES - 1, 1)

        def loads(t, parity):
            return 8 * (t - parity) + 16

        def free_slots(eng, t, j):
            slots = range(SLOT[j], SLOT[j] + MAIN[j])
            if j == STEPS - 1:
                eng.wait_ge(rounds_done, N_ROUND * t + last_round(slots) + 1)
            elif not is_first(t):
                eng.wait_ge(rounds_done, N_ROUND * (t - 1) + last_round_any(slots) + 1)

        def is_first(t):
            return isinstance(t, int) and t == 0

        def has_before(t, n):
            return not isinstance(t, int) or t >= n

        def is_last(t):
            return isinstance(t, int) and t == TILES - 1

        block = ctx.enter_context(nc.Block())

        @block.sync
        def _(sp):
            sp.dma_start(idx[:, 0, :], ids_t[0]).then_inc(idx_loaded[0], 16)
            sp.dma_start(idx[:, 1, :], ids_t[1]).then_inc(idx_loaded[1], 16)
            sp.dma_start(w_rows[:, :], Ws.rearrange("l o e -> (l o) e")).then_inc(weights_loaded, 16)
            sp.dma_start(vec_rows[0:4, :], b_top1.rearrange("(c p) -> c p", p=P)).then_inc(weights_loaded, 16)
            sp.dma_start(vec_rows[4:6, :], b_top2.rearrange("(c p) -> c p", p=P)).then_inc(weights_loaded, 16)
            sp.dma_start(vec_rows[6:8, :], W_top3.rearrange("(c p) o -> c (p o)", p=P)).then_inc(weights_loaded, 16)
            sp.dma_start(bias_all[:, :], bs.rearrange("l o -> (l o)").partition_broadcast(P)).then_inc(weights_loaded, 16)
            sp.dma_start(w1[:, :], W_top1).then_inc(weights_loaded, 16)
            sp.dma_start(w2[:, :, :], W_top2.rearrange("(c p) n -> p c n", p=P)).then_inc(weights_loaded, 16)
            sp.dma_start(h[:, 0, LAYERS * F:H_IN], ctx_t[0]).then_inc(ctx_loaded[0], 16)
            sp.dma_start(h[:, 1, LAYERS * F:H_IN], ctx_t[1]).then_inc(ctx_loaded[1], 16)

            def tile(t, parity):
                sp.wait_ge(turned, STEPS * t + STEPS)
                sp.dma_start(idx[:, parity, :], ids_t[t + 2]).then_inc(idx_loaded[parity], 16)
                sp.wait_ge(h_turned, t + 1)
                sp.dma_start(h[:, parity, LAYERS * F:H_IN], ctx_t[t + 2]).then_inc(ctx_loaded[parity], 16)

            with sp.Fori(0, TILES // 2 - 1) as pair:
                tile(2 * pair, 0)
                tile(2 * pair + 1, 1)
            sp.wait_ge(score_copied, TILES)
            sp.dma_start(out.rearrange("b o -> o b"), score[:, :]).then_inc(out_written, 16)
            sp.wait_ge(out_written, 16)

        @block.gpsimd
        def _(pool):
            pool.memset(ident[:, :], 0.0).then_inc(zeroed, 1)
            pool.wait_ge(zeroed, 1)
            pool.affine_select(out=ident[:, :], in_=ident[:, :], compare_op=ALU.not_equal, fill=1.0,
                               base=0, pattern=[[-1, P]], channel_multiplier=1).then_inc(ident_ready, 1)

            def gather(parity, j):
                for f in (2 * j, 2 * j + 1):
                    pool.indirect_dma_start(
                        out=rows[:, f, :], out_offset=None, in_=tables[f],
                        in_offset=bass.IndirectOffsetOnAxis(ap=idx[:, parity, f:f + 1], axis=0),
                    ).then_inc(rows_landed[j], 16)

            def multiply(t, parity, j):
                n = POOL_G[j]
                new_x = xt[:, parity, 2 * j:2 * j + 2, :]
                old_x = xt[:, parity, 0:n, :]
                out_ = prod[:, SLOT[j]:SLOT[j] + MAIN[j], :].rearrange("p (f g) e -> p f g e", f=2)[:, :, 0:n, :]
                if n == 1:
                    pool.tensor_tensor(out_[:, :, 0, :], old_x.to_broadcast([P, 2, FE]), new_x,
                                       ALU.mult).then_inc(pool_mult, 1)
                else:
                    pool.tensor_tensor(out_, old_x.unsqueeze(1).to_broadcast([P, 2, n, FE]),
                                       new_x.unsqueeze(2).to_broadcast([P, 2, n, FE]),
                                       ALU.mult).then_inc(pool_mult, 1)

            def tile(t, parity):
                gathered = 0
                for j in range(STEPS):
                    if POOL_G[j]:
                        if gathered == 0 and not is_last(t):
                            pool.wait_ge(idx_loaded[1 - parity], loads(t + 1, 1 - parity))
                        pool.wait_ge(copied, STEPS * t + j + 1)
                        free_slots(pool, t, j)
                        multiply(t, parity, j)
                        if not is_last(t):
                            for g in range(gathered, j + 1):
                                gather(1 - parity, g)
                            gathered = j + 1
                pool.wait_ge(copied, STEPS * t + STEPS)
                need(pool, rounds_done, N_ROUND * t)
                by_pair = xt[:, parity, :, :].rearrange("p (j two) e -> p j two e", two=2)
                pool.tensor_tensor(odd[:, :, :], by_pair[:, :, 0, :], by_pair[:, :, 1, :],
                                   ALU.mult).then_inc(pool_mult, 1)

            pool.wait_ge(idx_loaded[0], 16)
            for j in range(STEPS):
                gather(0, j)
            over_tiles(pool, tile)

        @block.scalar
        def _(act):
            act.wait_ge(setup_step, 2)
            act.wait_ge(setup_turned, 1)
            for half in range(HALVES):
                turned_w = mlp[:, half * 64:half * 64 + LAYERS * F]
                act.copy(w0[:, half, 0, 0:F], turned_w[:, 0:F])
                act.copy(w0[:, half, 1, F:2 * F], turned_w[:, 0:F])
                act.mul(w0_half[:, half, F:2 * F], turned_w[:, 0:F], 0.5)
                act.copy(w12[:, half, :], turned_w[:, F:3 * F])
            act.copy(vec[:, :], mlp[:, P:P + 8]).then_inc(setup_copied, 1)

            def features(t, parity, j):
                act.wait_ge(turned, STEPS * t + j + 1)
                if j == 0 and has_before(t, 2):
                    act.wait_ge(projected, t - 1)
                    act.wait_ge(pool_mult, N_POOL * (t - 1))
                act.copy(xt[:, parity, 2 * j:2 * j + 2, :], x_ps[j % XBANKS][:, :, :]).then_inc(copied, 1)

            def squares(t, parity, q):
                if q == 0:
                    need(act, rounds_done, N_ROUND * (t - 1) + DIAG_ROUND + 1 if has_before(t, 1) else 0)
                act.wait_ge(copied, STEPS * t + 2 * q + 2)
                act.activation(diag[:, 4 * q:4 * q + 4, :], xt[:, parity, 4 * q:4 * q + 4, :],
                               ACT.Square).then_inc(squared, 1)

            def relu_bank(t, k):
                act.wait_ge(rounds_done, N_ROUND * t + BANK_ROUND[k] + 1)
                if k == 0 and has_before(t, 1):
                    act.wait_ge(z0_summed, t)
                n = BANK_COLS[k] // P
                act.activation(relu0[:, GROUP * k:GROUP * k + n, :].rearrange("p n b -> p (n b)"),
                               acc[ACC_OF_BANK[k]][:, 0:BANK_COLS[k]], ACT.Relu,
                               bias=bias_bank[:, max(k - 2, 0):max(k - 2, 0) + 1], scale=2.0).then_inc(relued, 1)

            def copy_pt(t):
                act.wait_ge(projected, t + 1)
                need(act, p_ready, t)
                act.copy(pt[:, :], acc[ACC_OF_PT][:, :]).then_inc(pt_copied, 1)

            def sum_layer(t, parity, layer, half):
                act.wait_ge(y_ready, 4 * t + 2 * (layer - 1) + half + 1)
                for i in range(F // 2):
                    o = layer * F + half * (F // 2) + i
                    last = act.activation(y[:, half, :, i, :], y[:, half, :, i, :], ACT.Relu,
                                          bias=bias_all[:, o:o + 1], accum_out=h[:, parity, o:o + 1])
                last.then_inc(y_summed, 1)

            def copy_h(t):
                act.wait_ge(h_turned, t + 1)
                act.copy(h_t[:, :], mlp[0:H_IN, 0:P]).then_inc(h_copied, 1)

            def relu_hid1(t):
                act.wait_ge(hid1_ready, t + 1)
                for c in range(H1 // P):
                    last = act.activation(hid1[:, c, :], mlp[:, c * P:(c + 1) * P], ACT.Relu, bias=vec[:, c:c + 1])
                last.then_inc(hid1_relued, 1)

            def relu_hid2(t):
                act.wait_ge(hid2_ready, t + 1)
                for c in range(H2 // P):
                    last = act.activation(hid2[:, c, :], mlp[:, c * P:(c + 1) * P], ACT.Relu, bias=vec[:, 4 + c:5 + c])
                last.then_inc(hid2_relued, 1)

            def copy_score(t):
                act.wait_ge(score_ready, t + 1)
                act.copy(score[:, bass.ts(t, P)], mlp[0:1, 0:P]).then_inc(score_copied, 1)

            def tile(t, parity):
                for j in range(STEPS):
                    if j + 3 < STEPS:
                        features(t, parity, j + 3)
                    elif not is_last(t):
                        features(t + 1, 1 - parity, j + 3 - STEPS)
                    if has_before(t, 1):
                        if j == 0:
                            relu_bank(t - 1, 3)
                            relu_bank(t - 1, 4)
                        if j == 3:
                            sum_layer(t - 1, 1 - parity, 1, 0)
                        if j == 4:
                            sum_layer(t - 1, 1 - parity, 1, 1)
                        if j == 7:
                            sum_layer(t - 1, 1 - parity, 2, 0)
                    if has_before(t, 2):
                        if j == 2:
                            copy_h(t - 2)
                        if j == 3:
                            relu_hid1(t - 2)
                        if j == 4:
                            relu_hid2(t - 2)
                        if j == 5:
                            copy_score(t - 2)
                    if 3 <= j <= 6:
                        squares(t, parity, j - 3)
                    if j == 5:
                        relu_bank(t, 0)
                    if j == 6:
                        relu_bank(t, 1)
                        copy_pt(t)
                    if j == 7:
                        relu_bank(t, 2)
                        if has_before(t, 1):
                            sum_layer(t - 1, 1 - parity, 2, 1)

            for j in range(3):
                features(0, 0, j)
            act.wait_ge(setup_step, SETUP_STEPS)
            over_tiles(act, tile)
            t = TILES - 1
            relu_bank(t, 3)
            relu_bank(t, 4)
            for step in (copy_h, relu_hid1, relu_hid2, copy_score):
                step(t - 1)
            for layer in (1, 2):
                for half in range(2):
                    sum_layer(t, 1, layer, half)
            for step in (copy_h, relu_hid1, relu_hid2, copy_score):
                step(t)

        @block.vector
        def _(dve):
            dve.memset(w0[:, :, :, :], 0.0).then_inc(setup_step, 1)
            dve.memset(w0_half[:, :, :], 0.0).then_inc(setup_step, 1)
            dve.memset(h[:, :, H_IN:P], 0.0)
            steps = [2]

            def link(instruction):
                instruction.then_inc(setup_step, 1)
                steps[0] += 1
                dve.wait_ge(setup_step, steps[0])

            dve.wait_ge(ident_ready, 1)
            dve.wait_ge(weights_loaded, 16 * 7)
            link(dve.tensor_reduce(fold[:, :], ident[:, :].rearrange("p (k o) -> p o k", o=F), AX_X, ALU.add))
            link(dve.tensor_reduce(second[:, :], ident[:, :].rearrange("p (k o) -> p k o", o=2 * F)[:, :, F:2 * F],
                                   mybir.AxisListType.XY, ALU.add))
            link(dve.tensor_tensor(bias_masked[:, :], fold[:, :], bias_all[:, 0:F], ALU.mult))
            link(dve.tensor_reduce(bias0[:, :], bias_masked[:, :], AX_X, ALU.add))
            link(dve.tensor_tensor(bias0_2nd[:, :], bias0[:, :], second[:, :], ALU.mult))
            link(dve.tensor_scalar(bias_bank[:, 0:1], bias0[:, :], 2.0, None, ALU.mult))
            link(dve.tensor_tensor(bias_bank[:, 1:2], bias_bank[:, 0:1], bias0_2nd[:, :], ALU.subtract))
            link(dve.tensor_tensor(bias_bank[:, 2:3], bias_bank[:, 1:2], bias0_2nd[:, :], ALU.subtract))
            assert steps[0] == SETUP_STEPS

            def multiply(t, parity, j):
                dve.wait_ge(copied, STEPS * t + j + 1)
                free_slots(dve, t, j)
                g0, g1 = POOL_G[j], 2 * j
                n = g1 - g0
                out_ = prod[:, SLOT[j]:SLOT[j] + MAIN[j], :].rearrange("p (f g) e -> p f g e", f=2)[:, :, g0:g1, :]
                a = xt[:, parity, g0:g1, :].unsqueeze(1).to_broadcast([P, 2, n, FE])
                b = x_ps[j % XBANKS][:, :, :].unsqueeze(2).to_broadcast([P, 2, n, FE])
                dve.tensor_tensor(out_, a, b, ALU.mult).then_inc(dve_mult, 1)

            def copy_z0(t, parity):
                dve.wait_ge(z0_summed, t + 1)
                dve.wait_ge(ctx_loaded[parity], loads(t, parity))
                dve.tensor_copy(h[:, parity, 0:F], mlp[:, 0:F]).then_inc(z0_ready, 1)

            def scale_layer(t, parity, layer, half):
                if layer == 1 and half == 0:
                    dve.wait_ge(z0_ready, t + 1)
                    dve.wait_ge(p_ready, t + 1)
                    need(dve, y_summed, 4 * t)
                if layer == 2 and half == 0:
                    dve.wait_ge(y_summed, 4 * t + 2)
                ho = F // 2
                a = p_ps[:, :, layer - 1, half * ho:(half + 1) * ho, :].rearrange("p c o i -> p c (o i)")
                b = h[:, parity, (layer - 1) * F:layer * F]
                dve.tensor_tensor(y[:, half, :, :, :].rearrange("p c o (i g) -> p c (o i) g", g=F),
                                  a.unsqueeze(3).to_broadcast([P, F // 4, ho * 4, F]),
                                  b.unsqueeze(1).unsqueeze(1).to_broadcast([P, F // 4, ho * 4, F]),
                                  ALU.mult).then_inc(y_ready, 1)

            def tile(t, parity):
                for j in range(STEPS):
                    if has_before(t, 1) and j == 2:
                        copy_z0(t - 1, 1 - parity)
                    if j > 0:
                        multiply(t, parity, j)
                    if has_before(t, 1):
                        if j == 2:
                            scale_layer(t - 1, 1 - parity, 1, 0)
                        if j == 3:
                            scale_layer(t - 1, 1 - parity, 1, 1)
                        if j == 6:
                            scale_layer(t - 1, 1 - parity, 2, 0)
                            scale_layer(t - 1, 1 - parity, 2, 1)

            over_tiles(dve, tile)
            t = TILES - 1
            copy_z0(t, 1)
            for layer in (1, 2):
                for half in range(2):
                    scale_layer(t, 1, layer, half)

        @block.tensor
        def _(pe):
            pe.wait_ge(weights_loaded, 16 * 7)
            pe.wait_ge(ident_ready, 1)
            for half in range(HALVES):
                pe.transpose(mlp[:, half * 64:half * 64 + LAYERS * F], w_rows[:, half * P:(half + 1) * P],
                             ident[0:LAYERS * F, 0:LAYERS * F])
            pe.transpose(mlp[:, P:P + 8], vec_rows[:, :], ident[0:8, 0:8]).then_inc(setup_turned, 1)

            def turn(t, j):
                pe.wait_ge(rows_landed[j], 32 * t + 32)
                if j >= XBANKS or has_before(t, 1):
                    before = t if j >= XBANKS else t - 1
                    jb = (j - XBANKS) % STEPS
                    pe.wait_ge(copied, STEPS * before + jb + 1)
                    if jb > 0:
                        pe.wait_ge(dve_mult, N_DVE * before + jb)
                for f in range(2):
                    for half in range(HALVES):
                        last = pe.transpose(x_ps[j % XBANKS][:, f, half * P:(half + 1) * P],
                                            rows[:, 2 * j + f, half * P:(half + 1) * P], ident[:, :])
                last.then_inc(turned, 1)

            def bank_free(t, k):
                if k == 0:
                    need(pe, relued, BANKS * (t - 1) + 4 if has_before(t, 1) else 0)
                elif k == 1:
                    need(pe, relued, BANKS * t)
                elif k == 2:
                    pe.wait_ge(relued, BANKS * t + 2)
                elif k == 3:
                    pe.wait_ge(pt_copied, t + 1)
                elif k == 4:
                    pe.wait_ge(relued, BANKS * t + 3)

            def contract(t, k, place, groups, weights, cols):
                for half in range(HALVES):
                    for c in range(4):
                        last = pe.matmul(acc[ACC_OF_BANK[k]][32 * c:32 * c + 32, 0:cols], weights[:, half, :],
                                         groups[c][:, :, half * P:(half + 1) * P],
                                         start=(place == 0 and half == 0),
                                         stop=((place == 1 or k == BANKS - 1) and half == HALVES - 1),
                                         tile_position=(0, 32 * c))
                last.then_inc(rounds_done, 1)

            def product_round(t, r):
                j = ROUND_STEP[r]
                pe.wait_ge(dve_mult, N_DVE * t + j)
                pe.wait_ge(pool_mult, N_POOL * t + pool_done(j))
                if r % 2 == 0:
                    bank_free(t, r // 2)
                groups = [prod[:, GROUP_SLOT[4 * r + c]:GROUP_SLOT[4 * r + c] + GROUP, :] for c in range(4)]
                contract(t, r // 2, r % 2, groups, w0[:, :, r % 2, :], GROUP * P)

            def diag_round(t):
                pe.wait_ge(squared, 4 * t + 4)
                contract(t, 3, 1, [diag[:, 4 * c:4 * c + 4, :] for c in range(4)], w0_half, GROUP * P)

            def odd_round(t):
                pe.wait_ge(pool_mult, N_POOL * t + N_POOL)
                bank_free(t, 4)
                contract(t, 4, 0, [odd[:, 2 * c:2 * c + 2, :] for c in range(4)], w0[:, :, 0, :], 2 * P)

            def project(t, parity):
                pe.wait_ge(copied, STEPS * t + STEPS)
                pe.wait_ge(relued, BANKS * t + 1)
                for half in range(HALVES):
                    for c in range(4):
                        last = pe.matmul(acc[ACC_OF_PT][32 * c:32 * c + 32, :], w12[:, half, :],
                                         xt[:, parity, 4 * c:4 * c + 4, half * P:(half + 1) * P],
                                         start=(half == 0), stop=(half == HALVES - 1), tile_position=(0, 32 * c))
                last.then_inc(projected, 1)

            def turn_pt(t):
                pe.wait_ge(pt_copied, t + 1)
                need(pe, y_ready, 4 * t)
                for i in range(4):
                    last = pe.transpose(p_ps[:, :, :, :, i].rearrange("p c l o -> p (c l o)"),
                                        pt[:, i * P:(i + 1) * P], ident[:, :])
                last.then_inc(p_ready, 1)

            def sum_z0(t):
                pe.wait_ge(relued, BANKS * (t + 1))
                for n in range(SUM_SLOTS):
                    last = pe.matmul(mlp[:, 0:F], relu0[:, n, :], fold[:, :], start=(n == 0), stop=(n == SUM_SLOTS - 1))
                last.then_inc(z0_summed, 1)

            def turn_h(t, parity, newest):
                pe.wait_ge(y_summed, 4 * t + 4)
                pe.wait_ge(ctx_loaded[parity], loads(t, parity))
                pe.wait_ge(z0_ready, newest + 1)
                pe.transpose(mlp[:, 0:P], h[:, parity, :], ident[:, :]).then_inc(h_turned, 1)

            def top1(t):
                pe.wait_ge(h_copied, t + 1)
                for c in range(H1 // P):
                    last = pe.matmul(mlp[:, c * P:(c + 1) * P], w1[:, c * P:(c + 1) * P], h_t[:, :],
                                     start=True, stop=True)
                last.then_inc(hid1_ready, 1)

            def top2(t):
                pe.wait_ge(hid1_relued, t + 1)
                for m in range(H2 // P):
                    for c in range(H1 // P):
                        last = pe.matmul(mlp[:, m * P:(m + 1) * P], w2[:, c, m * P:(m + 1) * P], hid1[:, c, :],
                                         start=(c == 0), stop=(c == H1 // P - 1))
                last.then_inc(hid2_ready, 1)

            def top3(t):
                pe.wait_ge(hid2_relued, t + 1)
                for c in range(H2 // P):
                    last = pe.matmul(mlp[0:1, 0:P], vec[:, 6 + c:7 + c], hid2[:, c, :],
                                     start=(c == 0), stop=(c == H2 // P - 1))
                last.then_inc(score_ready, 1)

            def tile(t, parity):
                for j in range(STEPS):
                    if j + 3 < STEPS:
                        turn(t, j + 3)
                    elif not is_last(t):
                        turn(t + 1, j + 3 - STEPS)
                    if has_before(t, 1) and j == 1:
                        sum_z0(t - 1)
                    if has_before(t, 2):
                        if j == 2:
                            turn_h(t - 2, parity, t - 1)
                        if j == 3:
                            top1(t - 2)
                        if j == 4:
                            top2(t - 2)
                        if j == 5:
                            top3(t - 2)
                    for r in range(ROUNDS):
                        if ROUND_STEP[r] == j:
                            product_round(t, r)
                            if r == 3:
                                project(t, parity)
                diag_round(t)
                turn_pt(t)
                odd_round(t)

            for j in range(3):
                turn(0, j)
            pe.wait_ge(setup_copied, 1)
            pe.wait_ge(setup_step, SETUP_STEPS)
            over_tiles(pe, tile)
            t = TILES - 1
            sum_z0(t)
            turn_h(t - 1, 0, t)
            top1(t - 1)
            top2(t - 1)
            top3(t - 1)
            turn_h(t, 1, t)
            top1(t)
            top2(t)
            top3(t)


_TABLES = [f"tbl_{f}" for f in range(F)]
_INS = ["dense_ctx", "ids", *_TABLES, "W_top1", "b_top1", "W_top2", "b_top2", "W_top3", "L0_rec_Ws", "L0_rec_bs"]


def kernel(**inputs):
    import numpy as np
    import concourse.bacc as bacc
    from concourse.bass_utils import run_bass_kernel_spmd

    nc = bacc.Bacc("TRN2", target_bir_lowering=False, num_devices=1)
    arrays, args = {}, {}
    for name in _INS:
        a = np.ascontiguousarray(inputs[name])
        arrays[f"in_{name}"] = a
        args[name] = nc.dram_tensor(f"in_{name}", a.shape, mybir.dt.from_np(a.dtype), kind="ExternalInput").ap()
    out = nc.dram_tensor("out", (B, 1), F32, kind="ExternalOutput").ap()
    build(nc, args["dense_ctx"], args["ids"], [args[n] for n in _TABLES], args["W_top1"], args["b_top1"],
          args["W_top2"], args["b_top2"], args["W_top3"], args["L0_rec_Ws"], args["L0_rec_bs"], out)
    r = run_bass_kernel_spmd(nc, [arrays], core_ids=[0])
    return r.results[0]["out"]
```

```python
from contextlib import ExitStack

import concourse.bass as bass
from concourse import mybir

ALU = mybir.AluOpType
ACT = mybir.ActivationFunctionType
F32 = mybir.dt.float32
I32 = mybir.dt.int32
AX_X = mybir.AxisListType.X

P = 128
B = 1024
F = 16
E = 256
HALVES = E // P
FE = HALVES * P
TILES = B // P
STEPS = F // 2
LAYERS = 3
CTX = 16
H_IN = LAYERS * F + CTX
H1 = 512
H2 = 256

MAIN = [4 * j for j in range(STEPS)]
RING = sum(MAIN[:STEPS - 1])
SLOT = [sum(MAIN[:j]) if j < STEPS - 1 else MAIN[1] + MAIN[2] for j in range(STEPS)]
GROUP = 4
GROUP_SLOT = [SLOT[j] + GROUP * i for j in range(STEPS) for i in range(MAIN[j] // GROUP)]
ROUNDS = len(GROUP_SLOT) // 4
ROUND_STEP = [min(j for j in range(STEPS) if sum(MAIN[:j + 1]) >= 4 * GROUP * (r + 1)) for r in range(ROUNDS)]
DIAG_ROUND = ROUNDS - 2
ODD_ROUND = ROUNDS + 1
N_ROUND = ROUNDS + 2
BANKS = 5
BANK_OF_PRODUCTS = [(0, 0), (0, 1), (1, 0), (1, 1), (2, 0), (2, 1), (3, 1)]
BANK_ROUND = [1, 3, 6, 7, ODD_ROUND]
BANK_COLS = [GROUP * P] * 4 + [2 * P]
SUM_SLOTS = sum(BANK_COLS) // P
POOL_G_FIRST = [0] * STEPS
POOL_G = [[0, 0, 1, 1, 2, 2, 3, 2], [0, 0, 1, 1, 2, 2, 2, 2]]
POOL_G_LAST = [0, 1, 2, 3, 3, 4, 4, 4]
GATHERED_AT = [[], [], [0], [1, 2], [3], [4], [], [5, 6, 7]]
N_DVE = STEPS
N_POOL = sum(g > 0 for g in POOL_G[0])
XBANKS = 4
ACC_OF_BANK = [0, 1, 1, 0, 1]
ACC_OF_PT = 0
SETUP_STEPS = 10
SHARED = 6
POOL_O = 5
SPLIT = 3


def pool_features(t, parity):
    if isinstance(t, int) and t in (0, TILES - 1):
        return POOL_G_LAST if t else POOL_G_FIRST
    return POOL_G[parity]


def pool_count(t, j):
    if isinstance(t, int) and t == 0:
        return 0
    g = POOL_G_LAST if isinstance(t, int) and t == TILES - 1 else POOL_G[0]
    return N_POOL * (t - 1) + sum(n > 0 for n in g[:j + 1])


def place(r):
    return r if r < DIAG_ROUND else r + 1


def rounds_of(slots):
    return [i // 4 for i, first in enumerate(GROUP_SLOT) if any(first <= s < first + GROUP for s in slots)]


def last_round(slots, before=ROUNDS):
    return place(max(r for r in rounds_of(slots) if r < before))


def build(nc, dense_ctx, ids, tables, W_top1, b_top1, W_top2, b_top2, W_top3, Ws, bs, out):
    with ExitStack() as ctx:
        def sb(name, shape, dt=F32):
            return ctx.enter_context(nc.sbuf_tensor(name, shape, dt))

        def ps(name, shape, dt=F32):
            return ctx.enter_context(nc.psum_tensor(name, shape, dt))

        def sem(name):
            return ctx.enter_context(nc.semaphore(name))

        idx = sb("idx", [P, 2, F], I32)
        rows = sb("rows", [P, F, E])
        xt = sb("xt", [P, 2, F, FE])
        prod = sb("prod", [P, RING, FE])
        diag = sb("diag", [P, F, FE])
        odd = sb("odd", [P, STEPS, FE])
        relu0 = sb("relu0", [P, SUM_SLOTS, P])
        pt = sb("pt", [P, GROUP * P])
        y = sb("y", [P, 2, F // 4, F // 2, 4 * F])
        p_sb = sb("p_sb", [P, F // 4, 2, F, 4])
        h = sb("h", [P, 2, P])
        ident = sb("ident", [P, P])
        fold = sb("fold", [P, 2 * F])
        z0_part = sb("z0_part", [P, P])
        second = sb("second", [P, 1])
        w_rows = sb("w_rows", [LAYERS * F, E])
        w0 = sb("w0", [P, HALVES, 2, 2 * F])
        w0_half = sb("w0_half", [P, HALVES, 2 * F])
        w12 = sb("w12", [P, HALVES, 2 * F])
        bias_all = sb("bias_all", [P, LAYERS * F])
        bias_masked = sb("bias_masked", [P, F])
        bias0 = sb("bias0", [P, 1])
        bias0_2nd = sb("bias0_2nd", [P, 1])
        bias_bank = sb("bias_bank", [P, 3])
        vec_rows = sb("vec_rows", [8, P])
        vec = sb("vec", [P, 8])
        w1 = sb("w1", [H_IN, H1])
        w2 = sb("w2", [P, H1 // P, H2])
        h_t = sb("h_t", [H_IN, P])
        hid1 = sb("hid1", [P, H1 // P, P])
        hid2 = sb("hid2", [P, H2 // P, P])
        score = sb("score", [1, B])

        x_ps = [ps(f"x_ps{i}", [P, 2, FE]) for i in range(XBANKS)]
        acc = [ps(f"acc{i}", [P, GROUP * P]) for i in range(2)]
        p_ps = ps("p_ps", [P, F // 4, 2, F, 4])
        mlp = ps("mlp", [P, H1])
        late_banks = [bank[:, :, :].rearrange("p f e -> p (f e)") for bank in x_ps[1:4]]

        idx_loaded = [sem(f"idx_loaded{i}") for i in range(2)]
        ctx_loaded = [sem(f"ctx_loaded{i}") for i in range(2)]
        weights_loaded = sem("weights_loaded")
        rows_landed = [sem(f"rows_landed{j}") for j in range(STEPS)]
        zeroed = sem("zeroed")
        ident_ready = sem("ident_ready")
        setup_turned = sem("setup_turned")
        setup_copied = sem("setup_copied")
        setup_step = sem("setup_step")
        turned = sem("turned")
        copied = sem("copied")
        squared = sem("squared")
        dve_mult = sem("dve_mult")
        pool_mult = sem("pool_mult")
        odd_mult = sem("odd_mult")
        rounds_done = sem("rounds_done")
        projected = sem("projected")
        relued = sem("relued")
        pt_copied = sem("pt_copied")
        z0_summed = sem("z0_summed")
        z0_copied = sem("z0_copied")
        z0_folded = sem("z0_folded")
        z0_ready = sem("z0_ready")
        p_ready = sem("p_ready")
        p_copied = sem("p_copied")
        y_ready = sem("y_ready")
        y_pooled = sem("y_pooled")
        y_summed = sem("y_summed")
        y_shared = sem("y_shared")
        h_turned = sem("h_turned")
        h_copied = sem("h_copied")
        hid1_ready = sem("hid1_ready")
        hid1_relued = sem("hid1_relued")
        hid2_ready = sem("hid2_ready")
        hid2_relued = sem("hid2_relued")
        zero_ready = sem("zero_ready")
        score_ready = sem("score_ready")
        score_copied = sem("score_copied")
        out_written = sem("out_written")

        ids_t = ids.rearrange("(t p) f -> t p f", p=P)
        ctx_t = dense_ctx.rearrange("(t p) c -> t p c", p=P)

        def need(eng, semaphore, value):
            if not isinstance(value, int) or value > 0:
                eng.wait_ge(semaphore, value)

        def over_tiles(eng, tile):
            for t in range(3):
                tile(t, t % 2)
            with eng.Fori(0, (TILES - 4) // 2) as pair:
                tile(2 * pair + 3, 1)
                tile(2 * pair + 4, 0)
            tile(TILES - 1, (TILES - 1) % 2)

        def loads(t, parity):
            return 8 * (t - parity) + 16

        def scaled(t, layer, half, i):
            if is_last(t):
                return 4 * t + 3 * (layer - 1) + (3 if half else 2 if i >= F // 4 else 1)
            return 4 * t + 2 * (layer - 1) + half + 1

        def pooled(t, layer):
            return is_last(t) or is_late(t) and layer == 2

        def slots_of(j, features, others):
            return [SLOT[j] + 2 * j * f + g for f in features for g in others]

        def free_slots(eng, t, j, slots):
            if j == STEPS - 1:
                eng.wait_ge(rounds_done, N_ROUND * t + last_round(slots, before=ROUNDS - 2) + 1)
            elif not is_first(t):
                eng.wait_ge(rounds_done, N_ROUND * (t - 1) + last_round(slots) + 1)

        def is_first(t):
            return isinstance(t, int) and t == 0

        def is_last(t):
            return isinstance(t, int) and t == TILES - 1

        def exists(t):
            return not isinstance(t, int) or 0 <= t < TILES

        def is_late(t):
            return isinstance(t, int) and t >= TILES - 2

        def late_count(t):
            return t - (TILES - 2)

        def mlp_bank(t):
            if isinstance(t, int) and t >= TILES - 3:
                return late_banks[t - (TILES - 3)]
            return mlp

        def tower(t, c):
            if is_last(t):
                return (late_banks[2], late_banks[0], acc[0], acc[1])[c][:, 0:P]
            return mlp_bank(t)[:, c * P:(c + 1) * P]

        def chunks(t, n, c):
            return n * t + (c + 1 if is_last(t) else n)

        block = ctx.enter_context(nc.Block())

        @block.sync
        def _(sp):
            sp.dma_start(idx[:, 0, :], ids_t[0]).then_inc(idx_loaded[0], 16)
            sp.dma_start(idx[:, 1, :], ids_t[1]).then_inc(idx_loaded[1], 16)
            sp.dma_start(w_rows[:, :], Ws.rearrange("l o e -> (l o) e")).then_inc(weights_loaded, 16)
            sp.dma_start(vec_rows[0:4, :], b_top1.rearrange("(c p) -> c p", p=P)).then_inc(weights_loaded, 16)
            sp.dma_start(vec_rows[4:6, :], b_top2.rearrange("(c p) -> c p", p=P)).then_inc(weights_loaded, 16)
            sp.dma_start(vec_rows[6:8, :], W_top3.rearrange("(c p) o -> c (p o)", p=P)).then_inc(weights_loaded, 16)
            sp.dma_start(bias_all[:, :], bs.rearrange("l o -> (l o)").partition_broadcast(P)).then_inc(weights_loaded, 16)
            sp.dma_start(w1[:, :], W_top1).then_inc(weights_loaded, 16)
            sp.dma_start(w2[:, :, :], W_top2.rearrange("(c p) n -> p c n", p=P)).then_inc(weights_loaded, 16)
            sp.dma_start(h[:, 0, LAYERS * F:H_IN], ctx_t[0]).then_inc(ctx_loaded[0], 16)
            sp.dma_start(h[:, 1, LAYERS * F:H_IN], ctx_t[1]).then_inc(ctx_loaded[1], 16)

            def load_idx(t, parity):
                sp.wait_ge(turned, STEPS * (t - 1))
                sp.dma_start(idx[:, parity, :], ids_t[t]).then_inc(idx_loaded[parity], 16)

            def load_ctx(t, parity):
                sp.wait_ge(h_turned, t - 1)
                sp.dma_start(h[:, parity, LAYERS * F:H_IN], ctx_t[t]).then_inc(ctx_loaded[parity], 16)

            load_idx(2, 0)
            load_idx(3, 1)
            with sp.Fori(0, TILES // 2 - 2) as pair:
                for parity in range(2):
                    load_idx(2 * pair + 4 + parity, parity)
                    load_ctx(2 * pair + 2 + parity, parity)
            load_ctx(TILES - 2, 0)
            load_ctx(TILES - 1, 1)
            sp.wait_ge(score_copied, TILES)
            sp.dma_start(out.rearrange("b o -> o b"), score[:, :]).then_inc(out_written, 16)
            sp.wait_ge(out_written, 16)

        @block.gpsimd
        def _(pool):
            pool.memset(ident[:, :], 0.0).then_inc(zeroed, 1)
            pool.wait_ge(zeroed, 1)
            pool.affine_select(out=ident[:, :], in_=ident[:, :], compare_op=ALU.not_equal, fill=1.0,
                               base=0, pattern=[[-1, P]], channel_multiplier=1).then_inc(ident_ready, 1)

            def gather(parity, j):
                for f in (2 * j, 2 * j + 1):
                    pool.indirect_dma_start(
                        out=rows[:, f, :], out_offset=None, in_=tables[f],
                        in_offset=bass.IndirectOffsetOnAxis(ap=idx[:, parity, f:f + 1], axis=0),
                    ).then_inc(rows_landed[j], 16)

            def multiply(t, parity, j):
                pool.wait_ge(copied, STEPS * t + j + 1)
                n = pool_features(t, parity)[j]
                free_slots(pool, t, j, slots_of(j, (0, 1), range(n)))
                new_x = xt[:, parity, 2 * j:2 * j + 2, :]
                old_x = xt[:, parity, 0:n, :]
                out_ = prod[:, SLOT[j]:SLOT[j] + MAIN[j], :].rearrange("p (f g) e -> p f g e", f=2)[:, :, 0:n, :]
                if n == 1:
                    pool.tensor_tensor(out_[:, :, 0, :], old_x.to_broadcast([P, 2, FE]), new_x,
                                       ALU.mult).then_inc(pool_mult, 1)
                else:
                    pool.tensor_tensor(out_, old_x.unsqueeze(1).to_broadcast([P, 2, n, FE]),
                                       new_x.unsqueeze(2).to_broadcast([P, 2, n, FE]),
                                       ALU.mult).then_inc(pool_mult, 1)

            def multiply_odd(t, parity):
                pool.wait_ge(copied, STEPS * t + STEPS)
                need(pool, rounds_done, N_ROUND * t)
                by_pair = xt[:, parity, :, :].rearrange("p (j two) e -> p j two e", two=2)
                pool.tensor_tensor(odd[:, :, :], by_pair[:, :, 0, :], by_pair[:, :, 1, :],
                                   ALU.mult).then_inc(odd_mult, 1)

            def tile(t, parity):
                for j in range(STEPS):
                    if j == 2 and exists(t + 1):
                        pool.wait_ge(idx_loaded[1 - parity], loads(t + 1, 1 - parity))
                    if pool_features(t, parity)[j]:
                        multiply(t, parity, j)
                    if j == STEPS - 1 and not is_first(t):
                        multiply_odd(t, parity)
                    if exists(t + 1):
                        for g in GATHERED_AT[j]:
                            if is_first(t):
                                pool.wait_ge(turned, g + 1)
                            gather(1 - parity, g)
                if is_first(t):
                    multiply_odd(t, parity)

            def scale_outputs(t, parity, layer):
                pool.wait_ge(p_copied, late_count(t) + 1)
                if layer == 1:
                    pool.wait_ge(z0_ready, t + 1)
                else:
                    pool.wait_ge(y_summed, 4 * t + 2)
                pool.wait_ge(y_shared, 2 * late_count(t) + layer - 1)
                a = p_sb[:, :, layer - 1, F - POOL_O:F, :].rearrange("p c o i -> p c (o i)")
                b = h[:, parity, (layer - 1) * F:layer * F]
                out_ = y[:, 1, :, F // 2 - POOL_O:F // 2, :].rearrange("p c o (i g) -> p c (o i) g", g=F)
                pool.tensor_tensor(out_, a.unsqueeze(3).to_broadcast([P, F // 4, POOL_O * 4, F]),
                                   b.unsqueeze(1).unsqueeze(1).to_broadcast([P, F // 4, POOL_O * 4, F]),
                                   ALU.mult).then_inc(y_pooled, 1)

            def finish(t, parity):
                scale_outputs(t - 1, 1 - parity, 2)
                scale_outputs(t, parity, 1)
                scale_outputs(t, parity, 2)

            pool.wait_ge(idx_loaded[0], 16)
            for j in range(STEPS):
                gather(0, j)
            over_tiles(pool, tile)
            finish(TILES - 1, (TILES - 1) % 2)

        @block.scalar
        def _(act):
            def copy_weights():
                act.wait_ge(setup_step, 2)
                act.wait_ge(setup_turned, 1)
                for half in range(HALVES):
                    turned_w = mlp[:, half * 64:half * 64 + LAYERS * F]
                    act.copy(w0[:, half, 0, 0:F], turned_w[:, 0:F])
                    act.copy(w0[:, half, 1, F:2 * F], turned_w[:, 0:F])
                    act.mul(w0_half[:, half, 0:F], turned_w[:, 0:F], 0.5)
                    act.copy(w12[:, half, :], turned_w[:, F:3 * F])
                act.copy(vec[:, :], mlp[:, P:P + 8]).then_inc(setup_copied, 1)

            def features(t, parity, j):
                act.wait_ge(turned, STEPS * t + j + 1)
                if j == 0 and exists(t - 2):
                    act.wait_ge(projected, t - 1)
                    act.wait_ge(odd_mult, t - 1)
                act.copy(xt[:, parity, 2 * j:2 * j + 2, :], x_ps[j % XBANKS][:, :, :]).then_inc(copied, 1)

            def squares(t, parity, q):
                if q == 0:
                    need(act, rounds_done, N_ROUND * (t - 1) + DIAG_ROUND + 1 if exists(t - 1) else 0)
                act.wait_ge(copied, STEPS * t + 2 * q + 2)
                act.activation(diag[:, 4 * q:4 * q + 4, :], xt[:, parity, 4 * q:4 * q + 4, :],
                               ACT.Square).then_inc(squared, 1)

            def relu_bank(t, k):
                act.wait_ge(rounds_done, N_ROUND * t + BANK_ROUND[k] + 1)
                if k == 0 and exists(t - 1):
                    act.wait_ge(z0_summed, t)
                n = BANK_COLS[k] // P
                act.activation(relu0[:, GROUP * k:GROUP * k + n, :].rearrange("p n b -> p (n b)"),
                               acc[ACC_OF_BANK[k]][:, 0:BANK_COLS[k]], ACT.Relu,
                               bias=bias_bank[:, max(k - 2, 0):max(k - 2, 0) + 1], scale=2.0).then_inc(relued, 1)

            def copy_pt(t):
                act.wait_ge(projected, t + 1)
                need(act, p_ready, t)
                act.copy(pt[:, :], acc[ACC_OF_PT][:, :]).then_inc(pt_copied, 1)

            def copy_z0_part(t):
                act.wait_ge(z0_summed, t + 1)
                act.copy(z0_part[:, :], mlp[:, 0:P]).then_inc(z0_copied, 1)

            def copy_z0(t, parity):
                act.wait_ge(z0_folded, t + 1)
                act.wait_ge(ctx_loaded[parity], loads(t, parity))
                act.copy(h[:, parity, 0:F], mlp[:, 0:F]).then_inc(z0_ready, 1)

            def copy_p(t):
                act.wait_ge(p_ready, t + 1)
                if is_last(t):
                    act.wait_ge(y_pooled, 1)
                act.copy(p_sb[:, :, :, :, :], p_ps[:, :, :, :, :]).then_inc(p_copied, 1)

            def sum_layer(t, parity, layer, half, first=0, end=F // 2, whole=True):
                for i in range(first, end):
                    if i == first or is_last(t) and half == 0 and i == F // 4:
                        act.wait_ge(y_ready, scaled(t, layer, half, i))
                    o = layer * F + half * (F // 2) + i
                    last = act.activation(y[:, half, :, i, :], y[:, half, :, i, :], ACT.Relu,
                                          bias=bias_all[:, o:o + 1], accum_out=h[:, parity, o:o + 1])
                if whole:
                    last.then_inc(y_summed, 1)

            def copy_h(t):
                act.wait_ge(h_turned, t + 1)
                act.copy(h_t[:, :], tower(t, 0)[0:H_IN, :]).then_inc(h_copied, 1)

            def relu_hid1(t):
                for c in range(H1 // P):
                    act.wait_ge(hid1_ready, chunks(t, H1 // P, c))
                    act.activation(hid1[:, c, :], tower(t, c), ACT.Relu,
                                   bias=vec[:, c:c + 1]).then_inc(hid1_relued, 1)

            def relu_hid2(t):
                for c in range(H2 // P):
                    act.wait_ge(hid2_ready, chunks(t, H2 // P, c))
                    act.activation(hid2[:, c, :], tower(t, c), ACT.Relu,
                                   bias=vec[:, 4 + c:5 + c]).then_inc(hid2_relued, 1)

            def copy_score(t):
                act.wait_ge(score_ready, t + 1)
                act.copy(score[:, bass.ts(t, P)], tower(t, 2)[0:1, :]).then_inc(score_copied, 1)

            def tile(t, parity):
                one, two, three = exists(t - 1), exists(t - 2), exists(t - 3)
                other = 1 - parity
                features(t, parity, 3)
                features(t, parity, 4)
                if three:
                    copy_h(t - 3)
                if one:
                    relu_bank(t - 1, 2)
                if two:
                    sum_layer(t - 2, parity, 1, 1)
                features(t, parity, 5)
                if three:
                    relu_hid1(t - 3)
                if one:
                    relu_bank(t - 1, 3)
                features(t, parity, 6)
                if one:
                    relu_bank(t - 1, 4)
                features(t, parity, 7)
                if three:
                    relu_hid2(t - 3)
                squares(t, parity, 0)
                if three:
                    copy_score(t - 3)
                if two:
                    sum_layer(t - 2, parity, 2, 0)
                if exists(t + 1):
                    features(t + 1, other, 0)
                squares(t, parity, 1)
                if one:
                    copy_z0_part(t - 1)
                relu_bank(t, 0)
                if two:
                    sum_layer(t - 2, parity, 2, 1, end=SPLIT, whole=False)
                if one:
                    copy_z0(t - 1, other)
                if is_last(t):
                    copy_p(t - 1)
                if two:
                    sum_layer(t - 2, parity, 2, 1, first=SPLIT)
                if is_last(t):
                    relu_bank(t, 1)
                    copy_h(t - 2)
                if exists(t + 1):
                    features(t + 1, other, 1)
                copy_pt(t)
                squares(t, parity, 2)
                if exists(t + 1):
                    features(t + 1, other, 2)
                    relu_bank(t, 1)
                squares(t, parity, 3)
                if one:
                    sum_layer(t - 1, other, 1, 0)

            def finish(t, parity):
                other = 1 - parity
                sum_layer(t - 1, other, 1, 1, end=F // 2 - SHARED)
                relu_bank(t, 2)
                relu_hid1(t - 2)
                relu_bank(t, 3)
                relu_bank(t, 4)
                sum_layer(t - 1, other, 2, 0)
                copy_p(t)
                sum_layer(t - 1, other, 2, 1, end=F // 2 - SHARED)
                relu_hid2(t - 2)
                copy_h(t - 1)
                sum_layer(t, parity, 1, 0)
                sum_layer(t, parity, 1, 1, end=F // 2 - SHARED)
                copy_score(t - 2)
                relu_hid1(t - 1)
                sum_layer(t, parity, 2, 0)
                relu_hid2(t - 1)
                sum_layer(t, parity, 2, 1, end=F // 2 - SHARED)
                copy_score(t - 1)
                copy_h(t)
                relu_hid1(t)
                relu_hid2(t)
                copy_score(t)

            for j in range(3):
                features(0, 0, j)
            copy_weights()
            act.wait_ge(setup_step, SETUP_STEPS)
            over_tiles(act, tile)
            finish(TILES - 1, (TILES - 1) % 2)

        @block.vector
        def _(dve):
            dve.memset(w0[:, :, :, :], 0.0).then_inc(setup_step, 1)
            dve.memset(w0_half[:, :, :], 0.0).then_inc(setup_step, 1)
            dve.memset(h[:, :, H_IN:P], 0.0)
            dve.memset(fold[:, F:2 * F], 0.0)
            steps = [2]

            def link(instruction):
                instruction.then_inc(setup_step, 1)
                steps[0] += 1
                dve.wait_ge(setup_step, steps[0])

            dve.wait_ge(ident_ready, 1)
            dve.wait_ge(weights_loaded, 16 * 7)
            link(dve.tensor_reduce(fold[:, 0:F], ident[:, :].rearrange("p (k o) -> p o k", o=F), AX_X, ALU.add))
            link(dve.tensor_reduce(second[:, :], ident[:, :].rearrange("p (k o) -> p k o", o=2 * F)[:, :, F:2 * F],
                                   mybir.AxisListType.XY, ALU.add))
            link(dve.tensor_tensor(bias_masked[:, :], fold[:, 0:F], bias_all[:, 0:F], ALU.mult))
            link(dve.tensor_reduce(bias0[:, :], bias_masked[:, :], AX_X, ALU.add))
            link(dve.tensor_tensor(bias0_2nd[:, :], bias0[:, :], second[:, :], ALU.mult))
            link(dve.tensor_scalar(bias_bank[:, 0:1], bias0[:, :], 2.0, None, ALU.mult))
            link(dve.tensor_tensor(bias_bank[:, 1:2], bias0[:, :], bias0_2nd[:, :], ALU.add))
            link(dve.scalar_tensor_tensor(out=bias_bank[:, 2:3], in0=bias0_2nd[:, :], scalar=-2.0,
                                          in1=bias_bank[:, 0:1], op0=ALU.mult, op1=ALU.add))
            assert steps[0] == SETUP_STEPS

            def multiply(t, parity, j, feature=None):
                dve.wait_ge(copied, STEPS * t + j + 1)
                g0, g1 = pool_features(t, parity)[j], 2 * j
                free_slots(dve, t, j, slots_of(j, (0, 1) if feature is None else (feature,), range(g0, g1)))
                n = g1 - g0
                out_ = prod[:, SLOT[j]:SLOT[j] + MAIN[j], :].rearrange("p (f g) e -> p f g e", f=2)[:, :, g0:g1, :]
                if feature is None:
                    a = xt[:, parity, g0:g1, :].unsqueeze(1).to_broadcast([P, 2, n, FE])
                    b = x_ps[j % XBANKS][:, :, :].unsqueeze(2).to_broadcast([P, 2, n, FE])
                    dve.tensor_tensor(out_, a, b, ALU.mult).then_inc(dve_mult, 1)
                else:
                    b = x_ps[j % XBANKS][:, feature:feature + 1, :].to_broadcast([P, n, FE])
                    dve.tensor_tensor(out_[:, feature, :, :], xt[:, parity, g0:g1, :], b, ALU.mult).then_inc(dve_mult, 1)

            def copy_z0_part(t):
                dve.wait_ge(z0_summed, t + 1)
                dve.tensor_copy(z0_part[:, :], mlp[:, 0:P]).then_inc(z0_copied, 1)

            def copy_z0(t, parity):
                dve.wait_ge(z0_folded, t + 1)
                dve.wait_ge(ctx_loaded[parity], loads(t, parity))
                dve.tensor_copy(h[:, parity, 0:F], mlp[:, 0:F]).then_inc(z0_ready, 1)

            def scale_layer(t, parity, layer, half):
                if layer == 1 and half == 0:
                    dve.wait_ge(z0_ready, t + 1)
                    dve.wait_ge(p_ready, t + 1)
                    if is_late(t):
                        dve.wait_ge(p_copied, late_count(t) + 1)
                if layer == 1:
                    need(dve, y_summed, 4 * t - 1 + half if exists(t - 1) else 0)
                    if half == 1 and is_last(t):
                        dve.wait_ge(y_shared, 2)
                if layer == 2 and half == 0:
                    dve.wait_ge(y_summed, 4 * t + 2)
                    if is_late(t):
                        dve.wait_ge(y_shared, 2 * late_count(t) + 1)
                if is_last(t) and half == 0:
                    pieces = [(0, F // 4), (F // 4, F // 4)]
                elif half == 1 and pooled(t, layer):
                    pieces = [(0, F // 2 - POOL_O)]
                else:
                    pieces = [(0, F // 2)]
                for i, n in pieces:
                    o = half * (F // 2) + i
                    a = p_ps[:, :, layer - 1, o:o + n, :].rearrange("p c o i -> p c (o i)")
                    b = h[:, parity, (layer - 1) * F:layer * F]
                    dve.tensor_tensor(y[:, half, :, i:i + n, :].rearrange("p c o (i g) -> p c (o i) g", g=F),
                                      a.unsqueeze(3).to_broadcast([P, F // 4, n * 4, F]),
                                      b.unsqueeze(1).unsqueeze(1).to_broadcast([P, F // 4, n * 4, F]),
                                      ALU.mult).then_inc(y_ready, 1)

            def share_layer(t, parity, layer):
                dve.wait_ge(zero_ready, 1)
                dve.wait_ge(y_ready, scaled(t, layer, 1, F // 2))
                if pooled(t, layer):
                    dve.wait_ge(y_pooled, 2 * late_count(t) + layer - 1)
                for i in range(F // 2 - SHARED, F // 2):
                    o = layer * F + F // 2 + i
                    last = dve.scalar_tensor_tensor(out=y[:, 1, :, i, :], in0=y[:, 1, :, i, :],
                                                    scalar=bias_all[:, o:o + 1],
                                                    in1=zero.unsqueeze(1).to_broadcast([P, F // 4, 4 * F]),
                                                    op0=ALU.add, op1=ALU.max, accum_out=h[:, parity, o:o + 1])
                last.then_inc(y_shared, 1)

            def tile(t, parity):
                one, two = exists(t - 1), exists(t - 2)
                other = 1 - parity
                if two:
                    scale_layer(t - 2, parity, 1, 1)
                multiply(t, parity, 1)
                multiply(t, parity, 2)
                multiply(t, parity, 3)
                if is_last(t):
                    multiply(t, parity, 4)
                if two:
                    scale_layer(t - 2, parity, 2, 0)
                if not is_last(t):
                    multiply(t, parity, 4)
                if two:
                    scale_layer(t - 2, parity, 2, 1)
                multiply(t, parity, 5)
                multiply(t, parity, 6)
                if is_last(t):
                    multiply(t, parity, 7, 0)
                if one:
                    scale_layer(t - 1, other, 1, 0)
                if not is_last(t):
                    multiply(t, parity, 7, 0)
                multiply(t, parity, 7, 1)

            def finish(t, parity):
                other = 1 - parity
                dve.memset(zero, 0.0).then_inc(zero_ready, 1)
                scale_layer(t - 1, other, 1, 1)
                share_layer(t - 1, other, 1)
                scale_layer(t - 1, other, 2, 0)
                scale_layer(t - 1, other, 2, 1)
                share_layer(t - 1, other, 2)
                copy_z0_part(t)
                copy_z0(t, parity)
                scale_layer(t, parity, 1, 0)
                scale_layer(t, parity, 1, 1)
                share_layer(t, parity, 1)
                scale_layer(t, parity, 2, 0)
                scale_layer(t, parity, 2, 1)
                share_layer(t, parity, 2)

            zero = x_ps[0][:, 0, 0:1]
            over_tiles(dve, tile)
            finish(TILES - 1, (TILES - 1) % 2)

        @block.tensor
        def _(pe):
            def turn_weights():
                pe.wait_ge(weights_loaded, 16 * 7)
                for half in range(HALVES):
                    pe.transpose(mlp[:, half * 64:half * 64 + LAYERS * F], w_rows[:, half * P:(half + 1) * P],
                                 ident[0:LAYERS * F, 0:LAYERS * F])
                pe.transpose(mlp[:, P:P + 8], vec_rows[:, :], ident[0:8, 0:8]).then_inc(setup_turned, 1)

            def turn(t, j):
                pe.wait_ge(rows_landed[j], 32 * t + 32)
                if j >= XBANKS or exists(t - 1):
                    before = t if j >= XBANKS else t - 1
                    jb = (j - XBANKS) % STEPS
                    pe.wait_ge(copied, STEPS * before + jb + 1)
                    if jb > 0:
                        pe.wait_ge(dve_mult, N_DVE * before + (jb if jb < STEPS - 1 else N_DVE))
                for f in range(2):
                    for half in range(HALVES):
                        last = pe.transpose(x_ps[j % XBANKS][:, f, half * P:(half + 1) * P],
                                            rows[:, 2 * j + f, half * P:(half + 1) * P], ident[:, :])
                last.then_inc(turned, 1)

            def bank_free(t, k):
                if k == 0:
                    need(pe, relued, BANKS * (t - 1) + 4 if exists(t - 1) else 0)
                elif k == 1:
                    need(pe, relued, BANKS * t)
                elif k == 2:
                    pe.wait_ge(relued, BANKS * t + 2)
                elif k == 3:
                    pe.wait_ge(pt_copied, t + 1)
                elif k == 4:
                    pe.wait_ge(relued, BANKS * t + 3)

            def contract(t, k, second_half, groups, weights, cols):
                for half in range(HALVES):
                    for c in range(4):
                        last = pe.matmul(acc[ACC_OF_BANK[k]][32 * c:32 * c + 32, 0:cols], weights[:, half, :],
                                         groups[c][:, :, half * P:(half + 1) * P],
                                         start=(not second_half and half == 0),
                                         stop=((second_half or k == BANKS - 1) and half == HALVES - 1),
                                         tile_position=(0, 32 * c))
                last.then_inc(rounds_done, 1)

            def product_round(t, r):
                j = ROUND_STEP[r]
                bank, second_half = BANK_OF_PRODUCTS[r]
                if is_first(t) and r == 0:
                    pe.wait_ge(setup_copied, 1)
                    pe.wait_ge(setup_step, SETUP_STEPS)
                pe.wait_ge(dve_mult, N_DVE * t + (N_DVE if r == ROUNDS - 1 else j))
                need(pe, pool_mult, pool_count(t, j))
                if not second_half:
                    bank_free(t, bank)
                groups = [prod[:, GROUP_SLOT[4 * r + c]:GROUP_SLOT[4 * r + c] + GROUP, :] for c in range(4)]
                contract(t, bank, second_half, groups, w0[:, :, second_half, :], GROUP * P)

            def diag_round(t):
                pe.wait_ge(squared, 4 * t + 4)
                bank_free(t, 3)
                contract(t, 3, 0, [diag[:, 4 * c:4 * c + 4, :] for c in range(4)], w0_half, GROUP * P)

            def odd_round(t):
                pe.wait_ge(odd_mult, t + 1)
                bank_free(t, 4)
                contract(t, 4, 0, [odd[:, 2 * c:2 * c + 2, :] for c in range(4)], w0[:, :, 0, :], 2 * P)

            def project(t, parity):
                pe.wait_ge(copied, STEPS * t + STEPS)
                pe.wait_ge(relued, BANKS * t + 1)
                for half in range(HALVES):
                    for c in range(4):
                        last = pe.matmul(acc[ACC_OF_PT][32 * c:32 * c + 32, :], w12[:, half, :],
                                         xt[:, parity, 4 * c:4 * c + 4, half * P:(half + 1) * P],
                                         start=(half == 0), stop=(half == HALVES - 1), tile_position=(0, 32 * c))
                last.then_inc(projected, 1)

            def turn_pt(t):
                pe.wait_ge(pt_copied, t + 1)
                need(pe, y_ready, 4 * t)
                for i in range(4):
                    last = pe.transpose(p_ps[:, :, :, :, i].rearrange("p c l o -> p (c l o)"),
                                        pt[:, i * P:(i + 1) * P], ident[:, :])
                last.then_inc(p_ready, 1)

            def sum_z0(t):
                pe.wait_ge(relued, BANKS * (t + 1))
                if exists(t - 2):
                    pe.wait_ge(score_copied, t - 2 if is_last(t) else t - 1)
                for n in range(SUM_SLOTS):
                    c = n % 4
                    last = pe.matmul(mlp[32 * c:32 * c + 32, 0:P], fold[:, :], relu0[:, n, :],
                                     start=(n < 4), stop=(n >= SUM_SLOTS - 4), tile_position=(0, 32 * c))
                last.then_inc(z0_summed, 1)

            def fold_z0(t):
                pe.wait_ge(z0_copied, t + 1)
                pe.matmul(mlp[:, 0:F], z0_part[:, :], fold[:, 0:F], start=True, stop=True).then_inc(z0_folded, 1)

            def turn_h(t, parity, newest):
                pe.wait_ge(ctx_loaded[parity], loads(t, parity))
                pe.wait_ge(y_summed, 4 * t + 4)
                if is_late(t):
                    pe.wait_ge(y_shared, 2 * late_count(t) + 2)
                if mlp_bank(t) is mlp:
                    pe.wait_ge(z0_ready, newest + 1)
                pe.transpose(tower(t, 0), h[:, parity, :], ident[:, :]).then_inc(h_turned, 1)

            def top1(t):
                pe.wait_ge(h_copied, t + 1)
                for c in range(H1 // P):
                    pe.matmul(tower(t, c), w1[:, c * P:(c + 1) * P], h_t[:, :],
                              start=True, stop=True).then_inc(hid1_ready, 1)

            def top2(t):
                for m in range(H2 // P):
                    for c in range(H1 // P):
                        if m == 0:
                            pe.wait_ge(hid1_relued, chunks(t, H1 // P, c))
                        last = pe.matmul(tower(t, m), w2[:, c, m * P:(m + 1) * P], hid1[:, c, :],
                                         start=(c == 0), stop=(c == H1 // P - 1))
                    last.then_inc(hid2_ready, 1)

            def top3(t):
                for c in range(H2 // P):
                    pe.wait_ge(hid2_relued, chunks(t, H2 // P, c))
                    last = pe.matmul(tower(t, 2)[0:1, :], vec[:, 6 + c:7 + c], hid2[:, c, :],
                                     start=(c == 0), stop=(c == H2 // P - 1))
                last.then_inc(score_ready, 1)

            def tile(t, parity):
                one, two, three = exists(t - 1), exists(t - 2), exists(t - 3)
                turn(t, 3)
                turn(t, 4)
                if one:
                    product_round(t - 1, 6)
                turn(t, 5)
                if three:
                    top1(t - 3)
                turn(t, 6)
                if one:
                    odd_round(t - 1)
                if three:
                    top2(t - 3)
                turn(t, 7)
                product_round(t, 0)
                if three:
                    top3(t - 3)
                if exists(t + 1):
                    turn(t + 1, 0)
                if one:
                    sum_z0(t - 1)
                product_round(t, 1)
                if one:
                    turn_pt(t - 1)
                product_round(t, 2)
                if one:
                    fold_z0(t - 1)
                if exists(t + 1):
                    turn(t + 1, 1)
                project(t, parity)
                if exists(t + 1):
                    turn(t + 1, 2)
                product_round(t, 3)
                if is_last(t):
                    turn_h(t - 2, parity, t - 1)
                product_round(t, 4)
                if is_last(t):
                    top1(t - 2)
                if two and not is_last(t):
                    turn_h(t - 2, parity, t - 1)
                diag_round(t)
                if not is_last(t):
                    product_round(t, 5)

            def finish(t, parity):
                product_round(t, 5)
                product_round(t, 6)
                odd_round(t)
                turn_pt(t)
                sum_z0(t)
                top2(t - 2)
                fold_z0(t)
                turn_h(t - 1, 1 - parity, t)
                top3(t - 2)
                top1(t - 1)
                top2(t - 1)
                top3(t - 1)
                turn_h(t, parity, t)
                top1(t)
                top2(t)
                top3(t)

            pe.wait_ge(ident_ready, 1)
            for j in range(3):
                turn(0, j)
            turn_weights()
            over_tiles(pe, tile)
            finish(TILES - 1, (TILES - 1) % 2)


_TABLES = [f"tbl_{f}" for f in range(F)]
_INS = ["dense_ctx", "ids", *_TABLES, "W_top1", "b_top1", "W_top2", "b_top2", "W_top3", "L0_rec_Ws", "L0_rec_bs"]


def kernel(**inputs):
    import numpy as np
    import concourse.bacc as bacc
    from concourse.bass_utils import run_bass_kernel_spmd

    nc = bacc.Bacc("TRN2", target_bir_lowering=False, num_devices=1)
    arrays, args = {}, {}
    for name in _INS:
        a = np.ascontiguousarray(inputs[name])
        arrays[f"in_{name}"] = a
        args[name] = nc.dram_tensor(f"in_{name}", a.shape, mybir.dt.from_np(a.dtype), kind="ExternalInput").ap()
    out = nc.dram_tensor("out", (B, 1), F32, kind="ExternalOutput").ap()
    build(nc, args["dense_ctx"], args["ids"], [args[n] for n in _TABLES], args["W_top1"], args["b_top1"],
          args["W_top2"], args["b_top2"], args["W_top3"], args["L0_rec_Ws"], args["L0_rec_bs"], out)
    r = run_bass_kernel_spmd(nc, [arrays], core_ids=[0])
    return r.results[0]["out"]
```
